# Optimizing a Trainium2 kernel written in Bass

```python
import numpy as np
import jax
import jax.numpy as jnp

def _softmax(x, axis=-1):
    return jax.nn.softmax(x, axis=axis)

def _gelu(x):
    return jax.nn.gelu(x, approximate=True)

def _silu(x):
    return jax.nn.silu(x)

def _sigmoid(x):
    return jax.nn.sigmoid(x)

def _layernorm(x, axis=-1, eps=1e-05):
    m = jnp.mean(x, axis=axis, keepdims=True)
    v = jnp.var(x, axis=axis, keepdims=True)
    return (x - m) / jnp.sqrt(v + eps)

def _scatter_add(tgt, idx, src, axis=0):
    return tgt.at[idx].add(src)

def _segment_sum(src, seg, n):
    return jax.ops.segment_sum(src, seg, n)
kernel_name = 'mk_gnn_preln_d1_gnn_r8_5a63aa'

def setup_inputs(seed: int=0):
    np.random.seed(seed)
    _w = jnp.asarray

    def _rec_inputs():
        import jax
        import jax.numpy as jnp
        _gk = jax.random.key(seed)
        x = -0.000202 + 1 * jax.random.normal(jax.random.fold_in(_gk, 1), (6250, 128), jnp.float32)
        src = jax.random.randint(jax.random.fold_in(_gk, 2), (100000,), 0, 6250, jnp.int32)
        dst = jax.random.randint(jax.random.fold_in(_gk, 3), (100000,), 0, 6250, jnp.int32)
        _o = jnp.argsort(dst, stable=True)
        src = src[_o]
        dst = dst[_o]
        edge_attr_128 = -8.16379e-05 + 0.999858 * jax.random.normal(jax.random.fold_in(_gk, 12), (100000, 128), jnp.float32)
        return (x, src, dst, edge_attr_128)
    x, src, dst, edge_attr_128 = _rec_inputs()

    def _L0_gnn_setup():
        import jax, jax.numpy as jnp
        import numpy as np
        N_NODES = 6250
        N_EDGES = 100000
        D = 128
        RRELU_SLOPE = (1.0 / 8.0 + 1.0 / 3.0) / 2.0

        def _layer(h, edge_feats, src, dst, deg, iso, Wn, Ws, Wi, num_nodes):
            msg = (h[src] + edge_feats) @ Wn.T
            agg = jax.ops.segment_sum(msg, dst, num_segments=num_nodes)
            agg = agg / jnp.maximum(deg, 1.0)[:, None]
            self_msg = jnp.where(iso[:, None], h @ Wi.T, h @ Ws.T)
            x = agg + self_msg
            return jnp.where(x >= 0, x, RRELU_SLOPE * x)
        key = jax.random.key(seed)
        ks = jax.random.split(key, 10)
        s = 1.0 / np.sqrt(D)
        return {'node_feats': jax.random.normal(ks[0], (N_NODES, D), dtype=jnp.float32), 'edge_feats': jax.random.normal(ks[1], (N_EDGES, D), dtype=jnp.float32), 'src': jax.random.randint(ks[2], (N_EDGES,), 0, N_NODES, dtype=jnp.int32), 'dst': jax.random.randint(ks[3], (N_EDGES,), 0, N_NODES, dtype=jnp.int32), 'Wn0': jax.random.uniform(ks[4], (D, D), jnp.float32, -s, s), 'Ws0': jax.random.uniform(ks[5], (D, D), jnp.float32, -s, s), 'Wi0': jax.random.uniform(ks[6], (D, D), jnp.float32, -s, s), 'Wn1': jax.random.uniform(ks[7], (D, D), jnp.float32, -s, s), 'Ws1': jax.random.uniform(ks[8], (D, D), jnp.float32, -s, s), 'Wi1': jax.random.uniform(ks[9], (D, D), jnp.float32, -s, s)}
    _L0_gnn_all = _L0_gnn_setup()
    _L0_gnn_in = {k: v for k, v in _L0_gnn_all.items() if k in ('Wn0', 'Ws0', 'Wi0', 'Wn1', 'Ws1', 'Wi1')}
    del _L0_gnn_all
    return {'x': x, 'src': src, 'dst': dst, 'edge_attr_128': edge_attr_128, 'L0_gnn_Wn0': _L0_gnn_in['Wn0'], 'L0_gnn_Ws0': _L0_gnn_in['Ws0'], 'L0_gnn_Wi0': _L0_gnn_in['Wi0'], 'L0_gnn_Wn1': _L0_gnn_in['Wn1'], 'L0_gnn_Ws1': _L0_gnn_in['Ws1'], 'L0_gnn_Wi1': _L0_gnn_in['Wi1']}

def reference(x, src, dst, edge_attr_128, L0_gnn_Wn0, L0_gnn_Ws0, L0_gnn_Wi0, L0_gnn_Wn1, L0_gnn_Ws1, L0_gnn_Wi1):
    import jax
    import jax.numpy as jnp

    def _L0_gnn_ref(node_feats, edge_feats, src, dst, Wn0, Ws0, Wi0, Wn1, Ws1, Wi1):
        import jax, jax.numpy as jnp
        import numpy as np
        N_NODES = 6250
        N_EDGES = 100000
        D = 128
        RRELU_SLOPE = (1.0 / 8.0 + 1.0 / 3.0) / 2.0

        def _layer(h, edge_feats, src, dst, deg, iso, Wn, Ws, Wi, num_nodes):
            msg = (h[src] + edge_feats) @ Wn.T
            agg = jax.ops.segment_sum(msg, dst, num_segments=num_nodes)
            agg = agg / jnp.maximum(deg, 1.0)[:, None]
            self_msg = jnp.where(iso[:, None], h @ Wi.T, h @ Ws.T)
            x = agg + self_msg
            return jnp.where(x >= 0, x, RRELU_SLOPE * x)
        num_nodes = node_feats.shape[0]
        deg = jax.ops.segment_sum(jnp.ones(src.shape[0], dtype=node_feats.dtype), dst, num_segments=num_nodes)
        iso = deg == 0
        h = _layer(node_feats, edge_feats, src, dst, deg, iso, Wn0, Ws0, Wi0, num_nodes)
        h = _layer(h, edge_feats, src, dst, deg, iso, Wn1, Ws1, Wi1, num_nodes)
        return h
    h = jnp.maximum(_layernorm(x, axis=-1), 0.0)
    x = x + _L0_gnn_ref(h, edge_attr_128, src, dst, L0_gnn_Wn0, L0_gnn_Ws0, L0_gnn_Wi0, L0_gnn_Wn1, L0_gnn_Ws1, L0_gnn_Wi1)
    return x

_drawn_inputs = setup_inputs


def setup_inputs(seed=0):
    import zlib

    import numpy as np

    out = dict(_drawn_inputs(seed))
    spreads = {}
    factors = {}
    for name, (base, spread) in spreads.items():
        noise = np.random.default_rng([zlib.crc32(name.encode()), seed]).standard_normal(out[name].shape)
        drawn = base * np.exp(spread * noise) if base else spread * noise
        out[name] = jnp.asarray(drawn.astype(out[name].dtype))
    for name, factor in factors.items():
        out[name] = (out[name] * factor).astype(out[name].dtype)
    return out
```

```python
import concourse.bass as bass
from concourse import mybir
from contextlib import ExitStack


def gnn_program(nc, x, src, dst, edge_attr, Wn0, Ws0, Wi0, Wn1, Ws1, Wi1, out):
    fp32 = mybir.dt.float32
    i32 = mybir.dt.int32
    ALU = mybir.AluOpType
    ACT = mybir.ActivationFunctionType
    AX = mybir.AxisListType
    ds = bass.ds

    P = 128
    NODES, D = x.shape
    EDGES = src.shape[0]
    SLOTS = 16
    QUADS = 4
    QS = SLOTS // QUADS
    GROUP = P * SLOTS
    FULL = EDGES // GROUP
    GROUPS = -(-EDGES // GROUP)
    TAIL_P = (EDGES - FULL * GROUP) // SLOTS
    W = 160
    BLOCK = 256
    BLOCKS = -(-NODES // BLOCK)
    COLS = BLOCKS * BLOCK
    WINDOWS = COLS // W
    TAIL_N = NODES - (BLOCKS - 1) * BLOCK
    NB = 5
    SLOPE = (1.0 / 8.0 + 1.0 / 3.0) / 2.0
    EPS = 1e-5
    assert TAIL_P * SLOTS + FULL * GROUP == EDGES and GROUPS == FULL + 1
    assert COLS % W == 0 and BLOCKS % NB == 0 and TAIL_N % 2 == 0

    edge_full = edge_attr[0:FULL * GROUP, :].rearrange("(g p k) d -> p g (k d)", p=P, k=SLOTS)
    edge_tail = edge_attr[FULL * GROUP:EDGES, :].rearrange("(p k) d -> p (k d)", k=SLOTS)
    x_full = x[0:(BLOCKS - 1) * BLOCK, :].rearrange("(b p j) d -> p b (j d)", p=P, j=2)
    x_tail = x[(BLOCKS - 1) * BLOCK:NODES, :].rearrange("(p j) d -> p (j d)", j=2)
    out_full = out[0:(BLOCKS - 1) * BLOCK, :].rearrange("(b p j) d -> p b (j d)", p=P, j=2)
    out_tail = out[(BLOCKS - 1) * BLOCK:NODES, :].rearrange("(p j) d -> p (j d)", j=2)

    ctx = ExitStack()
    with ctx:
        def sb(name, shape, dt=fp32):
            return ctx.enter_context(nc.sbuf_tensor(name, shape, dt))

        def pb(name, shape):
            return ctx.enter_context(nc.psum_tensor(name, shape, fp32))

        def sem(name):
            return ctx.enter_context(nc.semaphore(name))

        h_dram = [nc.dram_tensor(f"h{layer}_rows", (COLS, D), fp32, kind="Internal").ap() for layer in range(2)]
        h_rows = [h.rearrange("(b p j) d -> p b (j d)", p=P, j=2) for h in h_dram]

        sums = sb("sums", [P, 3, COLS])
        hT = sb("hT", [P, COLS])
        x_sb = sb("x_sb", [P, BLOCKS, 2 * D])
        iota = sb("iota", [P, COLS])
        gath = sb("gath", [P, SLOTS, D])
        edge = sb("edge", [P, SLOTS, D])
        hot = sb("hot", [P, SLOTS, W])
        hot_sum = sb("hot_sum", [P, W])
        src_sb = sb("src_sb", [P, GROUPS, SLOTS], i32)
        dst_i = sb("dst_i", [P, GROUPS, SLOTS], i32)
        dst_sb = sb("dst_sb", [P, GROUPS, SLOTS])
        idx = sb("idx", [P, SLOTS], i32)
        ones = sb("ones", [P, P])
        ident = sb("ident", [P, P])
        w_raw = sb("w_raw", [P, 6, D])
        wT = sb("wT", [P, 6, D])

        mm_part = sb("mm_part", [P, 2, GROUPS])
        mm_group = sb("mm_group", [GROUPS, 2])
        base_f = sb("base_f", [1, 2, GROUPS])
        span = sb("span", [1, GROUPS])
        far = sb("far", [1, 2])
        base_i = sb("base_i", [1, GROUPS], i32)
        far_i = sb("far_i", [1, 1], i32)

        stats = sb("stats", [P, 2 * NB, 6])
        mv = sb("mv", [P, 2 * NB, 2])
        rstd = sb("rstd", [P, 2 * NB])
        nmr = sb("nmr", [P, 2 * NB])
        eps = sb("eps", [P, 1])
        h_row = sb("h_row", [P, 2 * NB, D])

        deg1 = sb("deg1", [P, BLOCK])
        lone = sb("lone", [P, BLOCK])
        mean = sb("mean", [P, BLOCK])
        h_lone = sb("h_lone", [P, BLOCK])
        h_met = sb("h_met", [P, BLOCK])
        act_in = sb("act_in", [P, BLOCK])
        made = sb("made", [P, BLOCK])
        y_rows = sb("y_rows", [P, 2, D])

        p_win = pb("p_win", [P, 3, 512])
        p_t = pb("p_t", [P, 2, 512])
        p_node = pb("p_node", [P, 512])

        s_x = sem("s_x")
        s_x_tail = sem("s_x_tail")
        s_dst = sem("s_dst")
        s_src = sem("s_src")
        s_w = sem("s_w")
        s_zero = sem("s_zero")
        s_id0 = sem("s_id0")
        s_ident = sem("s_ident")
        s_iota = sem("s_iota")
        s_dve = sem("s_dve")
        s_idx_pad = sem("s_idx_pad")
        s_mm_t = sem("s_mm_t")
        s_mm_g = sem("s_mm_g")
        s_mm_used = sem("s_mm_used")
        s_base_t = sem("s_base_t")
        s_base = sem("s_base")
        s_mv = sem("s_mv")
        s_std = sem("s_std")
        s_norm = sem("s_norm")
        s_hrow = sem("s_hrow")
        s_ln_t = sem("s_ln_t")
        s_ln_c = sem("s_ln_c")
        s_h0 = sem("s_h0")
        s_wt = sem("s_wt")
        s_wc = sem("s_wc")
        s_idx = sem("s_idx")
        s_gath = [sem(f"s_gath{q}") for q in range(QUADS)]
        s_edge = [sem(f"s_edge{q}") for q in range(QUADS)]
        s_hot = sem("s_hot")
        s_hot_sum = sem("s_hot_sum")
        s_used = sem("s_used")
        s_added = sem("s_added")
        x_hot = sem("x_hot")
        x_hot_sum = sem("x_hot_sum")
        x_idx = sem("x_idx")
        x_gath = sem("x_gath")
        x_edge = sem("x_edge")
        x_win = sem("x_win")
        x_added = sem("x_added")
        n_parts = sem("n_parts")
        n_prod = sem("n_prod")
        n_made = sem("n_made")
        n_hT = sem("n_hT")
        n_tr = sem("n_tr")
        n_rows = sem("n_rows")
        n_store = sem("n_store")
        s_out = sem("s_out")

        s_mark = sem("s_mark")

        def mark(engine):
            engine.sem_inc(s_mark, 1)

        block = ctx.enter_context(nc.Block())

        @block.sync
        def _(sp):
            sp.dma_start(x_sb[:, 0:BLOCKS - 1, :], x_full).then_inc(s_x, 16)
            sp.wait_ge(s_zero, 3)
            sp.dma_start(x_sb[0:TAIL_N // 2, BLOCKS - 1, :], x_tail).then_inc(s_x_tail, 16)
            for table, flat, s_loaded in ((dst_i, dst, s_dst), (src_sb, src, s_src)):
                sp.dma_start(table[:, 0:FULL, :], flat[0:FULL * GROUP].rearrange("(g p k) -> p g k", p=P, k=SLOTS)
                             ).then_inc(s_loaded, 16)
                sp.dma_start(table[0:TAIL_P, FULL, :], flat[FULL * GROUP:EDGES].rearrange("(p k) -> p k", k=SLOTS)
                             ).then_inc(s_loaded, 16)
            for n, w in enumerate((Wn0, Ws0, Wi0, Wn1, Ws1, Wi1)):
                sp.dma_start(w_raw[:, n, :], w).then_inc(s_w, 16)

            def load_edges(q, g):
                at = slice(q * QS * D, (q + 1) * QS * D)
                to = edge[:, q * QS:(q + 1) * QS, :].rearrange("p k d -> p (k d)")
                if g is None:
                    sp.dma_start(to[0:TAIL_P, :], edge_tail[:, at]).then_inc(s_edge[q], 16)
                else:
                    sp.dma_start(to, edge_full[:, ds(g, 1), at].rearrange("p g n -> p (g n)")).then_inc(s_edge[q], 16)

            for q in range(QUADS):
                load_edges(q, 0)
            with sp.Fori(1, FULL) as g:
                for q in range(QUADS):
                    sp.wait_ge(s_used, QUADS * g + (q + 1 - QUADS))
                    load_edges(q, g)
            for q in range(QUADS):
                sp.wait_ge(s_used, QUADS * (FULL - 1) + q + 1)
                load_edges(q, None)

            sp.wait_ge(s_base, 1)
            wide = sp.value_load(far_i[0:1, 0:1], min_val=0, max_val=1)
            with sp.If(wide != 0):
                sp.wait_ge(s_used, QUADS * GROUPS)
                whole = edge[:, :, :].rearrange("p k d -> p (k d)")
                sp.dma_start(whole, edge_full[:, 0, :]).then_inc(x_edge, 16)
                with sp.Fori(1, FULL) as g:
                    sp.wait_ge(x_win, g * (WINDOWS - 1))
                    sp.dma_start(whole, edge_full[:, ds(g, 1), :].rearrange("p g n -> p (g n)")).then_inc(x_edge, 16)
                sp.wait_ge(x_win, FULL * (WINDOWS - 1))
                sp.dma_start(whole[0:TAIL_P, :], edge_tail).then_inc(x_edge, 16)

            with sp.Fori(0, BLOCKS) as b:
                sp.wait_ge(n_rows, b + 1)
                sp.dma_start(h_rows[1][:, ds(b, 1), :].rearrange("p b n -> p (b n)"),
                             y_rows[:, :, :].rearrange("p j d -> p (j d)")).then_inc(n_store, 16)
            with sp.Fori(0, BLOCKS - 1) as b:
                sp.wait_ge(n_rows, b + (BLOCKS + 1))
                sp.dma_start(out_full[:, ds(b, 1), :].rearrange("p b n -> p (b n)"),
                             y_rows[:, :, :].rearrange("p j d -> p (j d)")).then_inc(n_store, 16)
            sp.wait_ge(n_rows, 2 * BLOCKS)
            sp.dma_start(out_tail, y_rows[0:TAIL_N // 2, :, :].rearrange("p j d -> p (j d)")).then_inc(n_store, 16)
            sp.wait_ge(n_store, 16 * 2 * BLOCKS)

        @block.gpsimd
        def _(pool):
            bound = pool.to_reg(COLS - 1)
            pool.memset(x_sb[:, BLOCKS - 1, :], 0.0).then_inc(s_zero, 1)
            pool.memset(src_sb[:, FULL, :], 0).then_inc(s_zero, 1)
            pool.memset(dst_i[:, FULL, :], -1).then_inc(s_zero, 1)
            pool.iota(iota[:, :], pattern=[[1, COLS]], base=0, channel_multiplier=0,
                      allow_small_or_imprecise_dtypes=True).then_inc(s_iota, 1)
            pool.memset(ident[:, :], 0.0).then_inc(s_id0, 1)
            pool.wait_ge(s_id0, 1)
            pool.affine_select(out=ident[:, :], in_=ident[:, :], compare_op=ALU.not_equal, fill=1.0,
                               base=0, pattern=[[-1, P]], channel_multiplier=1).then_inc(s_ident, 1)

            def gather(layer, k, s_done):
                pool.indirect_dma_start(
                    out=gath[:, k, :], out_offset=None, in_=h_dram[layer][:, :],
                    in_offset=bass.IndirectOffsetOnAxis(ap=idx[:, k:k + 1], axis=0),
                    bounds_check=bound, oob_is_err=False).then_inc(s_done, 16)

            pool.wait_ge(s_h0, 16 * BLOCKS // NB)
            for layer in range(2):
                if layer:
                    pool.wait_ge(n_store, 16 * BLOCKS)
                else:
                    for q in range(QUADS):
                        pool.wait_ge(s_idx, q + 1)
                        for k in range(q * QS, (q + 1) * QS):
                            gather(0, k, s_gath[q])
                with pool.Fori(0 if layer else 1, GROUPS) as g:
                    n = g + layer * GROUPS
                    for q in range(QUADS):
                        pool.wait_ge(s_idx, QUADS * n + (q + 1))
                        pool.wait_ge(s_used, QUADS * n + (q + 1 - QUADS))
                        mark(pool)
                        for k in range(q * QS, (q + 1) * QS):
                            gather(layer, k, s_gath[q])
                if not layer:
                    pool.wait_ge(s_base, 1)
                    wide = pool.value_load(far_i[0:1, 0:1], min_val=0, max_val=1)
                with pool.If(wide != 0):
                    pool.wait_ge(s_used, QUADS * GROUPS * (layer + 1))
                    with pool.Fori(0, GROUPS) as g:
                        pool.wait_ge(x_idx, g + (layer * GROUPS + 1))
                        mark(pool)
                        for k in range(SLOTS):
                            gather(layer, k, x_gath)

        @block.scalar
        def _(act):
            with act.Fori(0, BLOCKS // NB) as c:
                act.wait_ge(s_mv, c + 1)
                act.activation(rstd[:, :], mv[:, :, 1], ACT.Sqrt, bias=eps[:, :]).then_inc(s_std, 1)
                act.wait_ge(s_norm, c + 1)
                for t in range(2 * NB):
                    row = x_sb[:, ds(c * NB + t // 2, 1), (t % 2) * D:(t % 2 + 1) * D].rearrange("p b n -> p (b n)")
                    ins = act.activation(h_row[:, t, :], row, ACT.Relu,
                                         bias=nmr[:, t:t + 1], scale=rstd[:, t:t + 1])
                ins.then_inc(s_hrow, 1)
                act.wait_ge(s_hrow, c + 1)
                act.dma_start(h_rows[0][:, ds(c * NB, NB), :],
                              h_row[:, :, :].rearrange("p (b j) d -> p b (j d)", j=2)).then_inc(s_h0, 16)
                act.wait_ge(s_h0, 16 * c + 16)
                act.wait_ge(s_ln_t, NB * c + NB)

            def copy_indices(q, g, s_ready):
                act.activation(idx[:, q * QS:(q + 1) * QS],
                               src_sb[:, ds(g, 1), q * QS:(q + 1) * QS].rearrange("p g k -> p (g k)"),
                               ACT.Copy).then_inc(s_ready, 1)

            act.wait_ge(s_src, 32)
            for layer in range(2):
                if not layer:
                    for q in range(QUADS):
                        copy_indices(q, 0, s_idx)
                with act.Fori(0 if layer else 1, GROUPS) as g:
                    n = g + layer * GROUPS
                    for q in range(QUADS):
                        act.wait_ge(s_gath[q], 16 * QS * n)
                        copy_indices(q, g, s_idx)
                if not layer:
                    act.wait_ge(s_base, 1)
                    wide = act.value_load(far_i[0:1, 0:1], min_val=0, max_val=1)
                with act.If(wide != 0):
                    for q in range(QUADS):
                        act.wait_ge(s_gath[q], 16 * QS * GROUPS * (layer + 1))
                    with act.Fori(0, GROUPS) as g:
                        if layer:
                            act.wait_ge(x_win, (g + GROUPS) * (WINDOWS - 1))
                        else:
                            act.wait_ge(x_win, g * (WINDOWS - 1))
                        act.activation(idx[:, :], src_sb[:, ds(g, 1), :].rearrange("p g k -> p (g k)"),
                                       ACT.Copy).then_inc(x_idx, 1)
                with act.Fori(0, BLOCKS) as b:
                    m = b + layer * BLOCKS
                    act.wait_ge(n_prod, m + 1)
                    if layer:
                        act.wait_ge(s_out, m)
                    else:
                        act.wait_ge(s_out, b)
                    act.activation(made[:, :], p_node[:, 0:BLOCK], ACT.Copy).then_inc(n_made, 1)

        @block.vector
        def _(dve):
            chain = [0]

            def link(ins):
                chain[0] += 1
                ins.then_inc(s_dve, 1)
                dve.wait_ge(s_dve, chain[0])

            dve.memset(ones[:, :], 1.0).then_inc(s_dve, 1)
            dve.memset(eps[:, :], EPS).then_inc(s_dve, 1)
            dve.memset(sums[:, :, :], 0.0).then_inc(s_dve, 1)
            chain[0] = 3
            dve.wait_ge(s_dve, 3)

            dve.wait_ge(s_dst, 32)
            link(dve.tensor_copy(dst_sb[:, :, :], dst_i[:, :, :]))
            link(dve.tensor_reduce(mm_part[:, 1, :], dst_sb[:, :, :], AX.X, ALU.max))
            link(dve.tensor_scalar(dst_sb[:, FULL, :], dst_sb[:, FULL, :], 0.0, float(2 * COLS), ALU.is_lt, ALU.mult))
            link(dve.tensor_tensor(dst_sb[:, FULL, :], dst_sb[:, FULL, :], dst_i[:, FULL, :], ALU.add))
            link(dve.tensor_reduce(mm_part[:, 0, :], dst_sb[:, :, :], AX.X, ALU.min))
            dve.sem_inc(s_mm_t, 1)
            for i, op in enumerate((ALU.min, ALU.max)):
                dve.wait_ge(s_mm_g, i + 1)
                link(dve.tensor_reduce(mm_group[:, i:i + 1], p_t[0:GROUPS, i, 0:P], AX.X, op))
            dve.sem_inc(s_mm_used, 1)
            dve.wait_ge(s_base_t, 1)
            link(dve.tensor_copy(base_f[:, :, :], p_node[0:1, 0:2 * GROUPS].rearrange("o (i g) -> o i g", i=2)))
            link(dve.tensor_tensor(span[:, :], base_f[:, 1, :], base_f[:, 0, :], ALU.subtract))
            link(dve.tensor_reduce(far[:, 0:1], span[:, :], AX.X, ALU.max))
            link(dve.tensor_scalar(far[:, 0:1], far[:, 0:1], float(W) - 0.5, None, ALU.is_gt))
            link(dve.tensor_scalar(far[:, 1:2], far[:, 0:1], -1.0, 1.0, ALU.mult, ALU.add))
            link(dve.tensor_scalar(base_f[:, 0, :], base_f[:, 0, :], float(COLS - W), far[:, 1:2], ALU.min, ALU.mult))
            link(dve.tensor_copy(base_i[:, :], base_f[:, 0, :]))
            dve.tensor_copy(far_i[:, :], far[:, 0:1]).then_inc(s_base, 1)

            dve.wait_ge(s_x, 16)
            dve.wait_ge(s_x_tail, 16)
            hT_pairs = hT[:, :].rearrange("f (b p j) -> f b p j", p=P, j=2)
            with dve.Fori(0, BLOCKS // NB) as c:
                for t in range(2 * NB):
                    row = x_sb[:, ds(c * NB + t // 2, 1), (t % 2) * D:(t % 2 + 1) * D].rearrange("p b n -> p (b n)")
                    ins = dve.bn_stats(stats[:, t, :], row)
                ins.then_inc(s_dve, 1)
                dve.wait_ge(s_dve, c * 3 + (chain[0] + 1))
                mark(dve)
                for t in range(2 * NB):
                    ins = dve.bn_aggr(mv[:, t, :], stats[:, t, :])
                ins.then_inc(s_mv, 1)
                dve.wait_ge(s_std, c + 1)
                dve.reciprocal(rstd[:, :], rstd[:, :]).then_inc(s_dve, 1)
                dve.wait_ge(s_dve, c * 3 + (chain[0] + 2))
                dve.tensor_tensor(nmr[:, :], mv[:, :, 0], rstd[:, :], ALU.mult).then_inc(s_dve, 1)
                dve.wait_ge(s_dve, c * 3 + (chain[0] + 3))
                dve.tensor_scalar(nmr[:, :], nmr[:, :], -1.0, None, ALU.mult).then_inc(s_norm, 1)
                for t in range(NB):
                    dve.wait_ge(s_ln_t, c * NB + (t + 1))
                    dve.tensor_copy(hT_pairs[:, ds(c * NB + t, 1), :, :].rearrange("f b p j -> f j (b p)"),
                                    p_t[:, :, 0:P]).then_inc(s_ln_c, 1)
            chain[0] += 3 * (BLOCKS // NB)

            for i in range(2):
                dve.wait_ge(s_wt, i + 1)
                dve.tensor_copy(wT[:, 3 * i:3 * i + 3, :],
                                p_win[:, i, 0:3 * D].rearrange("p (n d) -> p n d", n=3)).then_inc(s_wc, 1)

            dve.wait_ge(s_iota, 1)

            def one_hots(q, g, start, s_ready):
                k = slice(q * QS, (q + 1) * QS)
                dve.tensor_tensor(
                    hot[:, k, :],
                    iota[:, ds(start, W)].unsqueeze(1).broadcast_to([P, QS, W]),
                    dst_sb[:, ds(g, 1), k].rearrange("p g k -> p (g k)").unsqueeze(2).broadcast_to([P, QS, W]),
                    ALU.is_equal).then_inc(s_ready, 1)

            def add_window(layer, start, s_done):
                if layer:
                    dve.tensor_tensor(sums[:, 1, ds(start, W)], sums[:, 1, ds(start, W)], p_win[:, 0, 0:W],
                                      ALU.add).then_inc(s_done, 1)
                else:
                    dve.tensor_tensor(sums[:, :, ds(start, W)], sums[:, :, ds(start, W)], p_win[:, :, 0:W],
                                      ALU.add).then_inc(s_done, 1)

            def base_of(g):
                return dve.value_load(base_i[0:1, ds(g, 1)], min_val=0, max_val=COLS - W)

            def group(layer, g, n, first=False):
                base = base_of(g)
                if not layer:
                    dve.wait_ge(s_hot_sum, g)
                for q in range(QUADS):
                    if not first:
                        dve.wait_ge(s_used, QUADS * n + (q + 1 - QUADS))
                    if q == QUADS - 1 and not first:
                        last = base_of(g - 1)
                        dve.wait_ge(s_used, QUADS * n)
                        add_window(layer, last, s_added)
                    one_hots(q, g, base, s_hot)
                if not layer:
                    dve.wait_ge(s_hot, QUADS * n + QUADS)
                    dve.tensor_reduce(hot_sum[:, :], hot[:, :, :].rearrange("p k w -> p w k"), AX.X,
                                      ALU.add).then_inc(s_hot_sum, 1)

            for layer in range(2):
                n0 = layer * GROUPS
                base = base_of(0)
                for q in range(QUADS):
                    one_hots(q, 0, base, s_hot)
                if not layer:
                    dve.wait_ge(s_hot, QUADS)
                    dve.tensor_reduce(hot_sum[:, :], hot[:, :, :].rearrange("p k w -> p w k"), AX.X,
                                      ALU.add).then_inc(s_hot_sum, 1)
                with dve.Fori(1, GROUPS) as g:
                    group(layer, g, g + n0)
                dve.wait_ge(s_used, QUADS * (n0 + GROUPS))
                add_window(layer, base_of(GROUPS - 1), s_added)
                dve.wait_ge(s_added, n0 + GROUPS)

                if not layer:
                    wide = dve.value_load(far_i[0:1, 0:1], min_val=0, max_val=1)
                with dve.If(wide != 0):
                    with dve.Fori(0, GROUPS) as g:
                        with dve.Fori(1, WINDOWS) as w:
                            m = (g + n0) * (WINDOWS - 1) + w
                            if layer:
                                dve.wait_ge(x_added, m - 1)
                            for q in range(QUADS):
                                one_hots(q, g, w * W, x_hot)
                            if not layer:
                                dve.wait_ge(x_hot, QUADS * m)
                                dve.tensor_reduce(hot_sum[:, :], hot[:, :, :].rearrange("p k w -> p w k"), AX.X,
                                                  ALU.add).then_inc(x_hot_sum, 1)
                            dve.wait_ge(x_win, m)
                            add_window(layer, w * W, x_added)
                            dve.wait_ge(x_added, m)

                with dve.Fori(0, BLOCKS) as b:
                    m = b + layer * BLOCKS
                    cols = ds(b * BLOCK, BLOCK)
                    step = 7 * m + chain[0]

                    def then(k, ins):
                        ins.then_inc(s_dve, 1)
                        dve.wait_ge(s_dve, step + k)

                    then(1, dve.tensor_scalar(lone[:, :], sums[:, 2, cols], 0.5, None, ALU.is_lt))
                    then(2, dve.tensor_scalar(deg1[:, :], sums[:, 2, cols], 1.0, None, ALU.max))
                    then(3, dve.reciprocal(deg1[:, :], deg1[:, :]))
                    if layer:
                        then(4, dve.tensor_copy(mean[:, :], sums[:, 1, cols]))
                    else:
                        then(4, dve.tensor_tensor(mean[:, :], sums[:, 0, cols], sums[:, 1, cols], ALU.add))
                    then(5, dve.tensor_tensor(mean[:, :], mean[:, :], deg1[:, :], ALU.mult))
                    then(6, dve.tensor_tensor(h_lone[:, :], hT[:, cols], lone[:, :], ALU.mult))
                    then(7, dve.tensor_tensor(h_met[:, :], hT[:, cols], h_lone[:, :], ALU.subtract))
                    dve.sem_inc(n_parts, 1)
                    dve.wait_ge(n_made, m + 1)
                    if not layer:
                        dve.scalar_tensor_tensor(hT[:, cols], made[:, :], SLOPE, made[:, :], ALU.mult, ALU.max).then_inc(n_hT, 1)
                    dve.scalar_tensor_tensor(act_in[:, :], made[:, :], SLOPE, made[:, :], ALU.mult, ALU.max).then_inc(s_out, 1)
                    dve.wait_ge(n_tr, m + 1)
                    if layer:
                        dve.wait_ge(n_store, 16 * m)
                        dve.tensor_tensor(y_rows[:, :, :], p_t[:, :, 0:D],
                                          x_sb[:, ds(b, 1), :].rearrange("p b (j d) -> p (b j) d", j=2),
                                          ALU.add).then_inc(n_rows, 1)
                    else:
                        dve.wait_ge(n_store, 16 * b)
                        dve.tensor_copy(y_rows[:, :, :], p_t[:, :, 0:D]).then_inc(n_rows, 1)

        @block.tensor
        def _(pe):
            pe.wait_ge(s_ident, 1)
            pe.wait_ge(s_mm_t, 1)
            for i in range(2):
                nc.tensor.transpose(p_t[0:GROUPS, i, 0:P], mm_part[:, i, :], ident[:, :]).then_inc(s_mm_g, 1)
            pe.wait_ge(s_mm_used, 1)
            for i in range(2):
                ins = nc.tensor.transpose(p_node[0:1, i * GROUPS:(i + 1) * GROUPS], mm_group[:, i:i + 1],
                                          ident[0:GROUPS, 0:GROUPS])
            ins.then_inc(s_base_t, 1)

            with pe.Fori(0, BLOCKS // NB) as c:
                pe.wait_ge(s_hrow, c + 1)
                for t in range(NB):
                    if t:
                        pe.wait_ge(s_ln_c, c * NB + t)
                    else:
                        pe.wait_ge(s_ln_c, c * NB)
                    for j in range(2):
                        ins = nc.tensor.transpose(p_t[:, j, 0:P], h_row[:, 2 * t + j, :], ident[:, :])
                    ins.then_inc(s_ln_t, 1)
            pe.wait_ge(s_w, 16 * 6)
            for i in range(2):
                for n in range(3):
                    ins = nc.tensor.transpose(p_win[:, i, n * D:(n + 1) * D], w_raw[:, 3 * i + n, :], ident[:, :])
                ins.then_inc(s_wt, 1)
            pe.wait_ge(s_wc, 2)

            def slot(layer, k):
                begin, end = k == 0, k == SLOTS - 1
                ins = nc.tensor.matmul(p_win[:, 0, 0:W], gath[:, k, :], hot[:, k, :], start=begin, stop=end)
                if not layer:
                    ins = nc.tensor.matmul(p_win[:, 1, 0:W], edge[:, k, :], hot[:, k, :], start=begin, stop=end)
                return ins

            def degree():
                return nc.tensor.matmul(p_win[:, 2, 0:W], ones[:, :], hot_sum[:, :], start=True, stop=True)

            for layer in range(2):
                n0 = layer * GROUPS
                with pe.Fori(0, GROUPS) as g:
                    n = g + n0
                    pe.wait_ge(s_added, n)
                    for q in range(QUADS):
                        pe.wait_ge(s_hot, QUADS * n + (q + 1))
                        pe.wait_ge(s_gath[q], 16 * QS * n + 16 * QS)
                        if not layer:
                            pe.wait_ge(s_edge[q], 16 * g + 16)
                        if q == QUADS - 1 and not layer:
                            pe.wait_ge(s_hot_sum, g + 1)
                            degree()
                        for k in range(q * QS, (q + 1) * QS):
                            ins = slot(layer, k)
                        ins.then_inc(s_used, 1)
                if not layer:
                    wide = pe.value_load(far_i[0:1, 0:1], min_val=0, max_val=1)
                with pe.If(wide != 0):
                    pe.wait_ge(s_added, n0 + GROUPS)
                    with pe.Fori(0, GROUPS) as g:
                        pe.wait_ge(x_gath, 16 * SLOTS * (g + (n0 + 1)))
                        if not layer:
                            pe.wait_ge(x_edge, 16 * g + 16)
                        mark(pe)
                        with pe.Fori(1, WINDOWS) as w:
                            m = (g + n0) * (WINDOWS - 1) + w
                            pe.wait_ge(x_hot, QUADS * m)
                            pe.wait_ge(x_added, m - 1)
                            if not layer:
                                pe.wait_ge(x_hot_sum, m)
                                degree()
                            for k in range(SLOTS):
                                ins = slot(layer, k)
                            ins.then_inc(x_win, 1)

                with pe.Fori(0, BLOCKS) as b:
                    m = b + layer * BLOCKS
                    pe.wait_ge(n_parts, m + 1)
                    for i, part in enumerate((mean, h_met, h_lone)):
                        ins = nc.tensor.matmul(p_node[:, 0:BLOCK], wT[:, 3 * layer + i, :], part[:, :],
                                               start=(i == 0), stop=(i == 2))
                    ins.then_inc(n_prod, 1)
                    pe.wait_ge(s_out, m + 1)
                    if layer:
                        pe.wait_ge(n_rows, m)
                    else:
                        pe.wait_ge(n_rows, b)
                    pairs = act_in[:, :].rearrange("f (p j) -> f p j", j=2)
                    for j in range(2):
                        ins = nc.tensor.transpose(p_t[:, j, 0:P], pairs[:, :, j], ident[:, :])
                    ins.then_inc(n_tr, 1)


_INS = ['x', 'src', 'dst', 'edge_attr_128', 'L0_gnn_Wn0', 'L0_gnn_Ws0', 'L0_gnn_Wi0',
        'L0_gnn_Wn1', 'L0_gnn_Ws1', 'L0_gnn_Wi1']


def kernel(**inputs):
    import numpy as _np
    import concourse.bacc as _bacc
    from concourse import mybir as _mybir
    from concourse.bass_utils import run_bass_kernel_spmd as _run

    nc = _bacc.Bacc("TRN2", target_bir_lowering=False, num_devices=1)
    arrays, args = {}, []
    for name in _INS:
        a = _np.ascontiguousarray(inputs[name])
        arrays[f"in_{name}"] = a
        args.append(nc.dram_tensor(f"in_{name}", a.shape, _mybir.dt.from_np(a.dtype), kind="ExternalInput").ap())
    args.append(nc.dram_tensor("out_0", inputs['x'].shape, _mybir.dt.float32, kind="ExternalOutput").ap())
    gnn_program(nc, *args)
    r = _run(nc, [arrays], core_ids=[0])
    return r.results[0]["out_0"]
```

```python
import concourse.bass as bass
from concourse import mybir
from contextlib import ExitStack


def gnn_program(nc, x, src, dst, edge_attr, Wn0, Ws0, Wi0, Wn1, Ws1, Wi1, out):
    fp32 = mybir.dt.float32
    i32 = mybir.dt.int32
    ALU = mybir.AluOpType
    ACT = mybir.ActivationFunctionType
    AX = mybir.AxisListType
    ds = bass.ds

    P = 128
    NODES, D = x.shape
    EDGES = src.shape[0]
    SLOTS = 16
    QUADS = 4
    QS = SLOTS // QUADS
    GROUP = P * SLOTS
    FULL = EDGES // GROUP
    GROUPS = -(-EDGES // GROUP)
    TAIL_P = (EDGES - FULL * GROUP) // SLOTS
    W = 160
    BLOCK = 256
    BLOCKS = -(-NODES // BLOCK)
    COLS = BLOCKS * BLOCK
    WINDOWS = COLS // W
    TAIL_N = NODES - (BLOCKS - 1) * BLOCK
    NB = 5
    STEPS = BLOCKS // NB
    PAIRS = (GROUPS - 1) // 2
    SLOPE = (1.0 / 8.0 + 1.0 / 3.0) / 2.0
    EPS = 1e-5
    assert TAIL_P * SLOTS + FULL * GROUP == EDGES and GROUPS == FULL + 1
    assert GROUPS == 1 + 2 * PAIRS and PAIRS == BLOCKS - 1
    assert COLS % W == 0 and BLOCKS % NB == 0 and TAIL_N % 2 == 0

    edge_full = edge_attr[0:FULL * GROUP, :].rearrange("(g p k) d -> p g (k d)", p=P, k=SLOTS)
    edge_tail = edge_attr[FULL * GROUP:EDGES, :].rearrange("(p k) d -> p (k d)", k=SLOTS)
    x_full = x[0:(BLOCKS - 1) * BLOCK, :].rearrange("(b p j) d -> p b (j d)", p=P, j=2)
    x_tail = x[(BLOCKS - 1) * BLOCK:NODES, :].rearrange("(p j) d -> p (j d)", j=2)
    out_full = out[0:(BLOCKS - 1) * BLOCK, :].rearrange("(b p j) d -> p b (j d)", p=P, j=2)
    out_tail = out[(BLOCKS - 1) * BLOCK:NODES, :].rearrange("(p j) d -> p (j d)", j=2)

    ctx = ExitStack()
    with ctx:
        def sb(name, shape, dt=fp32):
            return ctx.enter_context(nc.sbuf_tensor(name, shape, dt))

        def pb(name, shape):
            return ctx.enter_context(nc.psum_tensor(name, shape, fp32))

        def sem(name):
            return ctx.enter_context(nc.semaphore(name))

        h_dram = [nc.dram_tensor(f"h{layer}_rows", (COLS, D), fp32, kind="Internal").ap() for layer in range(2)]
        h_rows = [h.rearrange("(b p j) d -> p b (j d)", p=P, j=2) for h in h_dram]

        sums = sb("sums", [P, 3, COLS])
        hT = sb("hT", [P, COLS])
        x_sb = hT[:, :].rearrange("p (b n) -> p b n", n=2 * D)
        iota = sb("iota", [P, COLS])
        gath = sb("gath", [P, SLOTS, D])
        edge = sb("edge", [P, SLOTS, D])
        hot = sb("hot", [P, SLOTS, W])
        hot_sum = sb("hot_sum", [P, W])
        src_sb = sb("src_sb", [P, GROUPS, SLOTS], i32)
        dst_i = sb("dst_i", [P, GROUPS, SLOTS], i32)
        dst_sb = sb("dst_sb", [P, GROUPS, SLOTS])
        idx = sb("idx", [P, SLOTS], i32)
        ones = sb("ones", [P, P])
        ident = sb("ident", [P, P])
        w_raw = sb("w_raw", [P, 6, D])
        wT = sb("wT", [P, 6, D])

        ends_part = sb("ends_part", [P, 2, GROUPS])
        ends_group = sb("ends_group", [GROUPS, 2])
        ends = sb("ends", [1, 2, GROUPS])
        bound = sb("bound", [1, GROUPS])
        excess = sb("excess", [1, 2, GROUPS])
        mixed = sb("mixed", [1, 2])
        base_i = sb("base_i", [1, GROUPS], i32)
        mixed_i = sb("mixed_i", [1, 1], i32)

        stats = sb("stats", [P, 2 * BLOCKS, 6])
        mv = sb("mv", [P, 2 * BLOCKS, 2])
        std = sb("std", [P, 2 * BLOCKS])
        rstd = sb("rstd", [P, 2 * BLOCKS])
        shift = sb("shift", [P, 2 * BLOCKS])
        eps = sb("eps", [P, 1])

        row_in = sb("row_in", [P, 2, D])
        deg1 = sb("deg1", [P, BLOCK])
        rdeg = sb("rdeg", [P, BLOCK])
        total = sb("total", [P, BLOCK])
        mean = sb("mean", [P, BLOCK])
        h_lone = sb("h_lone", [P, BLOCK])
        h_met = sb("h_met", [P, BLOCK])
        made = sb("made", [P, BLOCK])
        act_out = sb("act_out", [P, BLOCK])
        y_rows = sb("y_rows", [P, 2, D])

        p_win = pb("p_win", [P, 3, 512])
        p_in = pb("p_in", [P, 2, 512])
        p_out = pb("p_out", [P, 2, 512])
        p_node = pb("p_node", [P, 512])

        s_x = [sem(f"s_x{c}") for c in range(STEPS)]
        s_x_pad = sem("s_x_pad")
        s_idx_pad = sem("s_idx_pad")
        s_dst = sem("s_dst")
        s_src = sem("s_src")
        s_w = sem("s_w")
        s_ident0 = sem("s_ident0")
        s_ident = sem("s_ident")
        s_iota = sem("s_iota")
        s_zeroed = sem("s_zeroed")
        s_eps = sem("s_eps")
        s_ends_part = sem("s_ends_part")
        s_ends_t = sem("s_ends_t")
        s_ends_group = sem("s_ends_group")
        s_ends = sem("s_ends")
        s_base = sem("s_base")
        s_wt = sem("s_wt")
        s_wc = sem("s_wc")
        s_mv = sem("s_mv")
        s_std = sem("s_std")
        s_shift = sem("s_shift")
        s_norm = sem("s_norm")
        s_h0 = sem("s_h0")
        s_chain = sem("s_chain")
        s_idx = sem("s_idx")
        s_gath = [sem(f"s_gath{q}") for q in range(QUADS)]
        s_edge = [sem(f"s_edge{q}") for q in range(QUADS)]
        s_hot = sem("s_hot")
        s_hot_sum = sem("s_hot_sum")
        s_used = sem("s_used")
        s_added = sem("s_added")
        x_idx = sem("x_idx")
        x_gath = sem("x_gath")
        x_edge = sem("x_edge")
        x_hot = sem("x_hot")
        x_hot_sum = sem("x_hot_sum")
        x_win = sem("x_win")
        x_added = sem("x_added")
        n_row_in = sem("n_row_in")
        n_in = sem("n_in")
        n_parts = sem("n_parts")
        n_prod = sem("n_prod")
        n_made = sem("n_made")
        n_act = sem("n_act")
        n_out = sem("n_out")
        n_rows = sem("n_rows")
        n_store = sem("n_store")
        s_mark = sem("s_mark")

        def mark(engine):
            engine.sem_inc(s_mark, 1)

        def general(engine):
            engine.wait_ge(s_base, 1)
            return engine.value_load(mixed_i[0:1, 0:1], min_val=0, max_val=1)

        block = ctx.enter_context(nc.Block())

        @block.sync
        def _(sp):
            for c in range(STEPS):
                if c < STEPS - 1:
                    sp.dma_start(x_sb[:, c * NB:(c + 1) * NB, :], x_full[:, c * NB:(c + 1) * NB, :]).then_inc(s_x[c], 16)
                else:
                    sp.dma_start(x_sb[:, c * NB:BLOCKS - 1, :], x_full[:, c * NB:BLOCKS - 1, :]).then_inc(s_x[c], 16)
                    sp.wait_ge(s_x_pad, 1)
                    sp.dma_start(x_sb[0:TAIL_N // 2, BLOCKS - 1, :], x_tail).then_inc(s_x[c], 16)
            for c in range(STEPS):
                sp.wait_ge(s_norm, c + 1)
                sp.dma_start(h_rows[0][:, c * NB:(c + 1) * NB, :], x_sb[:, c * NB:(c + 1) * NB, :]).then_inc(s_h0, 16)
            sp.wait_ge(s_h0, 16 * STEPS)

            def as_rows(buffer):
                return buffer[:, :, :].rearrange("p j d -> p (j d)")

            def load_rows(rows, b):
                sp.dma_start(as_rows(row_in), rows[:, ds(b, 1), :].rearrange("p b n -> p (b n)")).then_inc(n_row_in, 16)

            def load_edges(q, g, n):
                at = slice(q * QS * D, (q + 1) * QS * D)
                to = edge[:, q * QS:(q + 1) * QS, :].rearrange("p k d -> p (k d)")
                sp.wait_ge(s_used, QUADS * n + (q + 1))
                if g is None:
                    sp.dma_start(to[0:TAIL_P, :], edge_tail[:, at]).then_inc(s_edge[q], 16)
                else:
                    sp.dma_start(to, edge_full[:, ds(g, 1), at].rearrange("p g n -> p (g n)")).then_inc(s_edge[q], 16)

            def store_block(layer, b, more=True):
                m = b + layer * BLOCKS
                sp.wait_ge(n_rows, m + 1)
                to = h_rows[1] if layer == 0 else out_full
                sp.dma_start(to[:, ds(b, 1), :].rearrange("p b n -> p (b n)"), as_rows(y_rows)).then_inc(n_store, 16)
                sp.wait_ge(n_store, 16 * m + 16)
                if more:
                    load_rows(x_full if layer else h_rows[0], b + 1)

            def last_blocks(layer, b):
                store_block(layer, b, more=False)
                if layer:
                    sp.dma_start(row_in[0:TAIL_N // 2, :, :].rearrange("p j d -> p (j d)"), x_tail).then_inc(n_row_in, 16)
                    sp.wait_ge(n_rows, 2 * BLOCKS)
                    sp.dma_start(out_tail, y_rows[0:TAIL_N // 2, :, :].rearrange("p j d -> p (j d)")).then_inc(n_store, 16)
                    sp.wait_ge(n_store, 16 * 2 * BLOCKS)
                else:
                    load_rows(h_rows[0], b + 1)
                    store_block(0, b + 1, more=False)
                    load_rows(x_full, 0)

            load_rows(h_rows[0], 0)
            for q in range(QUADS):
                load_edges(q, 0, 0)
            mixed_sp = general(sp)
            with sp.If(mixed_sp == 0):
                with sp.Fori(1, 3) as g:
                    for q in range(QUADS):
                        load_edges(q, g, g)
                with sp.Fori(1, PAIRS - 1) as i:
                    for q in range(QUADS):
                        load_edges(q, 2 * i + 1, 2 * i + 1)
                    for q in range(QUADS):
                        load_edges(q, 2 * i + 2, 2 * i + 2)
                        if q == 2:
                            store_block(0, i - 1)
                for q in range(QUADS):
                    load_edges(q, FULL - 1, FULL - 1)
                for q in range(QUADS):
                    load_edges(q, None, FULL)
                    if q == 2:
                        store_block(0, BLOCKS - 3)
                last_blocks(0, BLOCKS - 2)
                with sp.Fori(0, BLOCKS - 2) as b:
                    store_block(1, b)
                last_blocks(1, BLOCKS - 2)
            with sp.If(mixed_sp != 0):
                with sp.Fori(1, FULL) as g:
                    for q in range(QUADS):
                        load_edges(q, g, g)
                for q in range(QUADS):
                    load_edges(q, None, FULL)
                whole = edge[:, :, :].rearrange("p k d -> p (k d)")
                sp.wait_ge(s_used, QUADS * (GROUPS + 1))
                with sp.Fori(0, FULL) as g:
                    sp.wait_ge(x_win, g * (WINDOWS - 1) + (WINDOWS - 1))
                    sp.dma_start(whole, edge_full[:, ds(g, 1), :].rearrange("p g n -> p (g n)")).then_inc(x_edge, 16)
                sp.wait_ge(x_win, (FULL + 1) * (WINDOWS - 1))
                sp.dma_start(whole[0:TAIL_P, :], edge_tail).then_inc(x_edge, 16)
                for layer in range(2):
                    with sp.Fori(0, BLOCKS - 2) as b:
                        store_block(layer, b)
                    last_blocks(layer, BLOCKS - 2)

        @block.gpsimd
        def _(pool):
            pool.memset(x_sb[:, BLOCKS - 1, :], 0.0).then_inc(s_x_pad, 1)
            pool.memset(src_sb[:, FULL, :], 0).then_inc(s_idx_pad, 1)
            pool.memset(dst_i[:, FULL, :], -1).then_inc(s_idx_pad, 1)
            pool.memset(ident[:, :], 0.0).then_inc(s_ident0, 1)
            pool.memset(bound[:, 0:1], 0.0)
            pool.iota(bound[:, 1:GROUPS].rearrange("o (i k) -> o i k", k=2), pattern=[[BLOCK, PAIRS], [0, 2]], base=0,
                      channel_multiplier=0, allow_small_or_imprecise_dtypes=True).then_inc(s_iota, 1)
            pool.wait_ge(s_ident0, 1)
            pool.affine_select(out=ident[:, :], in_=ident[:, :], compare_op=ALU.not_equal, fill=1.0,
                               base=0, pattern=[[-1, P]], channel_multiplier=1).then_inc(s_ident, 1)
            pool.iota(iota[:, :], pattern=[[1, COLS]], base=0, channel_multiplier=0,
                      allow_small_or_imprecise_dtypes=True).then_inc(s_iota, 1)
            pool.memset(sums[:, 0:2, :], 0.0).then_inc(s_zeroed, 1)
            top = pool.to_reg(COLS - 1)

            def gather(layer, k, s_done):
                pool.indirect_dma_start(
                    out=gath[:, k, :], out_offset=None, in_=h_dram[layer][:, :],
                    in_offset=bass.IndirectOffsetOnAxis(ap=idx[:, k:k + 1], axis=0),
                    bounds_check=top, oob_is_err=False).then_inc(s_done, 16)

            pool.wait_ge(s_h0, 16 * STEPS)
            mixed_pool = None
            for layer in range(2):
                if layer:
                    pool.wait_ge(n_store, 16 * BLOCKS)
                with pool.Fori(0, GROUPS) as g:
                    for q in range(QUADS):
                        pool.wait_ge(s_idx, QUADS * g + (QUADS * GROUPS * layer + q + 1))
                        mark(pool)
                        for k in range(q * QS, (q + 1) * QS):
                            gather(layer, k, s_gath[q])
                if not layer:
                    mixed_pool = general(pool)
                with pool.If(mixed_pool != 0):
                    with pool.Fori(0, GROUPS) as g:
                        pool.wait_ge(x_idx, g + (layer * GROUPS + 1))
                        mark(pool)
                        for k in range(SLOTS):
                            gather(layer, k, x_gath)

        @block.scalar
        def _(act):
            act.wait_ge(s_idx_pad, 2)
            for table, flat, s_loaded in ((src_sb, src, s_src), (dst_i, dst, s_dst)):
                act.dma_start(table[:, 0:FULL, :], flat[0:FULL * GROUP].rearrange("(g p k) -> p g k", p=P, k=SLOTS)
                              ).then_inc(s_loaded, 16)
                act.dma_start(table[0:TAIL_P, FULL, :], flat[FULL * GROUP:EDGES].rearrange("(p k) -> p k", k=SLOTS)
                              ).then_inc(s_loaded, 16)
            for n, w in enumerate((Wn0, Ws0, Wi0, Wn1, Ws1, Wi1)):
                act.dma_start(w_raw[:, n, :], w).then_inc(s_w, 16)

            def std_of(c):
                tiles = slice(2 * NB * c, 2 * NB * (c + 1))
                act.wait_ge(s_mv, c + 1)
                act.activation(std[:, tiles], mv[:, tiles, 1], ACT.Sqrt, bias=eps[:, :]).then_inc(s_std, 1)

            act.wait_ge(s_eps, 1)
            std_of(0)
            for c in range(STEPS):
                if c + 1 < STEPS:
                    std_of(c + 1)
                act.wait_ge(s_shift, c + 1)
                for t in range(2 * NB * c, 2 * NB * (c + 1)):
                    row = x_sb[:, t // 2, (t % 2) * D:(t % 2 + 1) * D]
                    ins = act.activation(row, row, ACT.Relu, bias=shift[:, t:t + 1], scale=rstd[:, t:t + 1])
                ins.then_inc(s_norm, 1)

            def indices(q, g, n):
                act.wait_ge(s_used, QUADS * n + (q + 1))
                act.activation(idx[:, q * QS:(q + 1) * QS],
                               src_sb[:, ds(g, 1), q * QS:(q + 1) * QS].rearrange("p g k -> p (g k)"),
                               ACT.Copy).then_inc(s_idx, 1)

            def product_out(m):
                act.wait_ge(n_prod, m + 1)
                act.activation(made[:, :], p_node[:, 0:BLOCK], ACT.Copy).then_inc(n_made, 1)

            act.wait_ge(s_src, 32)
            mixed_act = None
            for layer in range(2):
                n0, m0 = layer * GROUPS, layer * BLOCKS
                for q in range(QUADS):
                    indices(q, 0, n0)
                if not layer:
                    mixed_act = general(act)
                with act.If(mixed_act == 0):
                    with act.Fori(1, 3) as g:
                        for q in range(QUADS):
                            indices(q, g, g + n0)
                    with act.Fori(1, PAIRS) as i:
                        for q in range(QUADS):
                            indices(q, 2 * i + 1, 2 * i + (n0 + 1))
                        for q in range(QUADS):
                            indices(q, 2 * i + 2, 2 * i + (n0 + 2))
                            if q == 1:
                                product_out(i + (m0 - 1))
                    for b in (BLOCKS - 2, BLOCKS - 1):
                        product_out(b + m0)
                with act.If(mixed_act != 0):
                    with act.Fori(1, GROUPS) as g:
                        for q in range(QUADS):
                            indices(q, g, g + n0)
                    act.wait_ge(s_used, QUADS * (n0 + GROUPS + 1))
                    with act.Fori(0, GROUPS) as g:
                        act.wait_ge(x_win, g * (WINDOWS - 1) + (n0 + 1) * (WINDOWS - 1))
                        act.activation(idx[:, :], src_sb[:, ds(g, 1), :].rearrange("p g k -> p (g k)"),
                                       ACT.Copy).then_inc(x_idx, 1)
                    with act.Fori(0, BLOCKS) as b:
                        product_out(b + m0)

        @block.vector
        def _(dve):
            chain = [0]

            def link(ins):
                chain[0] += 1
                ins.then_inc(s_chain, 1)
                dve.wait_ge(s_chain, chain[0])

            dve.sem_inc(s_hot_sum, 1)
            dve.sem_inc(s_added, 1)
            dve.sem_inc(x_added, 1)
            dve.memset(eps[:, :], EPS).then_inc(s_eps, 1)
            link(dve.memset(ones[:, :], 1.0))

            def moments(c):
                dve.wait_ge(s_x[c], 32 if c == STEPS - 1 else 16)
                for t in range(2 * NB * c, 2 * NB * (c + 1)):
                    ins = dve.bn_stats(stats[:, t, :], x_sb[:, t // 2, (t % 2) * D:(t % 2 + 1) * D])
                link(ins)
                for t in range(2 * NB * c, 2 * NB * (c + 1)):
                    ins = dve.bn_aggr(mv[:, t, :], stats[:, t, :])
                ins.then_inc(s_mv, 1)

            moments(0)
            for c in range(STEPS):
                if c + 1 < STEPS:
                    moments(c + 1)
                tiles = slice(2 * NB * c, 2 * NB * (c + 1))
                dve.wait_ge(s_std, c + 1)
                link(dve.reciprocal(rstd[:, tiles], std[:, tiles]))
                dve.scalar_tensor_tensor(shift[:, tiles], mv[:, tiles, 0], -1.0, rstd[:, tiles],
                                         ALU.mult, ALU.mult).then_inc(s_shift, 1)

            dve.wait_ge(s_dst, 32)
            link(dve.tensor_copy(dst_sb[:, :, :], dst_i[:, :, :]))
            link(dve.tensor_reduce(ends_part[:, 1, :], dst_sb[:, :, :], AX.X, ALU.max))
            link(dve.tensor_scalar(dst_sb[:, FULL, :], dst_sb[:, FULL, :], 0.0, float(2 * COLS), ALU.is_lt, ALU.mult))
            link(dve.tensor_tensor(dst_sb[:, FULL, :], dst_sb[:, FULL, :], dst_i[:, FULL, :], ALU.add))
            dve.tensor_reduce(ends_part[:, 0, :], dst_sb[:, :, :], AX.X, ALU.min).then_inc(s_ends_part, 1)
            for i, op in enumerate((ALU.min, ALU.max)):
                dve.wait_ge(s_ends_t, i + 1)
                dve.tensor_reduce(ends_group[:, i:i + 1], p_in[0:GROUPS, i, 0:P], AX.X, op).then_inc(s_ends_group, 1)
            dve.wait_ge(s_ends, 1)
            link(dve.tensor_copy(ends[:, :, :], p_node[0:1, 0:2 * GROUPS].rearrange("o (i g) -> o i g", i=2)))
            dve.wait_ge(s_iota, 1)
            link(dve.scalar_tensor_tensor(excess[:, 0, :], ends[:, 1, :], float(1 - W), ends[:, 0, :],
                                          ALU.add, ALU.subtract))
            link(dve.tensor_tensor(excess[:, 1, :], bound[:, :], ends[:, 0, :], ALU.subtract))
            link(dve.tensor_reduce(mixed[:, 0:1], excess[:, :, :].rearrange("o i g -> o (i g)"), AX.X, ALU.max))
            link(dve.tensor_scalar(mixed[:, 0:1], mixed[:, 0:1], 0.5, None, ALU.is_gt))
            link(dve.tensor_scalar(mixed[:, 1:2], mixed[:, 0:1], -1.0, 1.0, ALU.mult, ALU.add))
            link(dve.tensor_scalar(ends[:, 0, :], ends[:, 0, :], float(COLS - W), mixed[:, 1:2], ALU.min, ALU.mult))
            link(dve.tensor_copy(base_i[:, :], ends[:, 0, :]))
            dve.tensor_copy(mixed_i[:, :], mixed[:, 0:1]).then_inc(s_base, 1)
            link(dve.memset(sums[:, 2, :], 0.0))
            dve.wait_ge(s_zeroed, 1)
            dve.wait_ge(s_iota, 2)

            def one_hots(q, g, start, s_ready):
                k = slice(q * QS, (q + 1) * QS)
                dve.tensor_tensor(
                    hot[:, k, :],
                    iota[:, ds(start, W)].unsqueeze(1).broadcast_to([P, QS, W]),
                    dst_sb[:, ds(g, 1), k].rearrange("p g k -> p (g k)").unsqueeze(2).broadcast_to([P, QS, W]),
                    ALU.is_equal).then_inc(s_ready, 1)

            def sum_hots(s_done):
                dve.tensor_reduce(hot_sum[:, :], hot[:, :, :].rearrange("p k w -> p w k"), AX.X,
                                  ALU.add).then_inc(s_done, 1)

            def add_window(layer, start, s_done):
                into = sums[:, 1, ds(start, W)] if layer else sums[:, :, ds(start, W)]
                dve.tensor_tensor(into, into, p_win[:, 0, 0:W] if layer else p_win[:, :, 0:W],
                                  ALU.add).then_inc(s_done, 1)

            def base_of(g):
                return dve.value_load(base_i[0:1, ds(g, 1)], min_val=0, max_val=COLS - W)

            def add_group(layer, g, n):
                base = base_of(g)
                dve.wait_ge(s_used, QUADS * n + 2 * QUADS)
                add_window(layer, base, s_added)

            def group(layer, g, n, first=False, after=()):
                base = base_of(g)
                if not layer:
                    dve.wait_ge(s_hot_sum, n + 1)
                for q in range(QUADS):
                    if q == QUADS - 1 and not first:
                        add_group(layer, g - 1, n - 1)
                    dve.wait_ge(s_used, QUADS * n + (q + 1))
                    one_hots(q, g, base, s_hot)
                    for at, step in after:
                        if at == q:
                            step()
                if not layer:
                    dve.wait_ge(s_hot, QUADS * n + QUADS)
                    sum_hots(s_hot_sum)

            def parts(layer, b):
                m = b + layer * BLOCKS
                cols = ds(b * BLOCK, BLOCK)
                if layer:
                    own = hT[:, cols]
                    dve.tensor_tensor(mean[:, :], sums[:, 1, cols], sums[:, 0, cols], ALU.mult)
                else:
                    dve.tensor_scalar(deg1[:, :], sums[:, 2, cols], 1.0, None, ALU.max).then_inc(s_chain, 1)
                    dve.tensor_tensor(total[:, :], sums[:, 0, cols], sums[:, 1, cols], ALU.add).then_inc(s_chain, 1)
                    dve.wait_ge(s_chain, 3 * b + (chain[0] + 2))
                    dve.reciprocal(rdeg[:, :], deg1[:, :]).then_inc(s_chain, 1)
                    dve.wait_ge(s_chain, 3 * b + (chain[0] + 3))
                    dve.tensor_tensor(mean[:, :], total[:, :], rdeg[:, :], ALU.mult)
                    dve.tensor_copy(sums[:, 0, cols], rdeg[:, :])
                    dve.wait_ge(n_in, b + 1)
                    own = p_in[:, :, 0:P].rearrange("f j p -> f p j")
                degree = sums[:, 2, cols]
                if not layer:
                    degree = degree.rearrange("f (p j) -> f p j", j=2)

                def shaped(t):
                    return t[:, :] if layer else t[:, :].rearrange("f (p j) -> f p j", j=2)

                dve.scalar_tensor_tensor(shaped(h_lone), degree, 0.5, own, ALU.is_lt, ALU.mult)
                dve.scalar_tensor_tensor(shaped(h_met), degree, 0.5, own, ALU.is_gt, ALU.mult).then_inc(n_parts, 1)

            def leaky(layer, b):
                dve.wait_ge(n_made, b + (layer * BLOCKS + 1))
                if not layer:
                    dve.scalar_tensor_tensor(hT[:, ds(b * BLOCK, BLOCK)], made[:, :], SLOPE, made[:, :],
                                             ALU.mult, ALU.max)
                dve.scalar_tensor_tensor(act_out[:, :], made[:, :], SLOPE, made[:, :],
                                         ALU.mult, ALU.max).then_inc(n_act, 1)

            def rows(layer, b):
                dve.wait_ge(n_out, b + (layer * BLOCKS + 1))
                if layer:
                    dve.wait_ge(n_row_in, 16 * b + 16 * (BLOCKS + 1))
                    dve.tensor_tensor(y_rows[:, :, :], p_out[:, :, 0:D], row_in[:, :, :], ALU.add).then_inc(n_rows, 1)
                else:
                    dve.tensor_copy(y_rows[:, :, :], p_out[:, :, 0:D]).then_inc(n_rows, 1)

            def weights_out():
                for i in range(2):
                    dve.wait_ge(s_wt, i + 1)
                    dve.tensor_copy(wT[:, 3 * i:3 * i + 3, :],
                                    (p_in, p_out)[i][:, 0, 0:3 * D].rearrange("p (n d) -> p n d", n=3)).then_inc(s_wc, 1)

            mixed_dve = None
            for layer in range(2):
                n0 = layer * GROUPS
                group(layer, 0, n0, first=True)
                if not layer:
                    weights_out()
                    mixed_dve = general(dve)
                with dve.If(mixed_dve == 0):
                    with dve.Fori(1, 3) as g:
                        group(layer, g, g + n0)
                    with dve.Fori(1, PAIRS) as i:
                        group(layer, 2 * i + 1, 2 * i + (n0 + 1))
                        dve.wait_ge(s_added, 2 * i + (n0 + 2))
                        parts(layer, i - 1)
                        group(layer, 2 * i + 2, 2 * i + (n0 + 2),
                              after=((1, lambda: leaky(layer, i - 1)), (2, lambda: rows(layer, i - 1))))
                    add_group(layer, GROUPS - 1, n0 + GROUPS - 1)
                    dve.wait_ge(s_added, n0 + GROUPS + 1)
                    for b in (BLOCKS - 2, BLOCKS - 1):
                        parts(layer, b)
                        leaky(layer, b)
                        rows(layer, b)
                with dve.If(mixed_dve != 0):
                    with dve.Fori(1, GROUPS) as g:
                        group(layer, g, g + n0)
                    add_group(layer, GROUPS - 1, n0 + GROUPS - 1)
                    dve.wait_ge(s_added, n0 + GROUPS + 1)
                    with dve.Fori(0, GROUPS) as g:
                        with dve.Fori(1, WINDOWS) as w:
                            m = (g + n0) * (WINDOWS - 1) + w
                            for q in range(QUADS):
                                one_hots(q, g, w * W, x_hot)
                            if not layer:
                                dve.wait_ge(x_hot, QUADS * m)
                                sum_hots(x_hot_sum)
                            dve.wait_ge(x_win, m + (WINDOWS - 1))
                            add_window(layer, w * W, x_added)
                            dve.wait_ge(x_added, m + 1)
                    with dve.Fori(0, BLOCKS) as b:
                        parts(layer, b)
                        leaky(layer, b)
                        rows(layer, b)
                if not layer:
                    chain[0] += 3 * BLOCKS

        @block.tensor
        def _(pe):
            pe.sem_inc(s_used, QUADS)
            pe.sem_inc(x_win, WINDOWS - 1)
            pe.wait_ge(s_ident, 1)
            pe.wait_ge(s_ends_part, 1)
            for i in range(2):
                nc.tensor.transpose(p_in[0:GROUPS, i, 0:P], ends_part[:, i, :], ident[:, :]).then_inc(s_ends_t, 1)
            pe.wait_ge(s_ends_group, 2)
            for i in range(2):
                ins = nc.tensor.transpose(p_node[0:1, i * GROUPS:(i + 1) * GROUPS], ends_group[:, i:i + 1],
                                          ident[0:GROUPS, 0:GROUPS])
            ins.then_inc(s_ends, 1)
            pe.wait_ge(s_w, 16 * 6)
            for i in range(2):
                for n in range(3):
                    ins = nc.tensor.transpose((p_in, p_out)[i][:, 0, n * D:(n + 1) * D], w_raw[:, 3 * i + n, :],
                                              ident[:, :])
                ins.then_inc(s_wt, 1)

            def slot(layer, k):
                begin, end = k == 0, k == SLOTS - 1
                ins = nc.tensor.matmul(p_win[:, 0, 0:W], gath[:, k, :], hot[:, k, :], start=begin, stop=end)
                if not layer:
                    ins = nc.tensor.matmul(p_win[:, 1, 0:W], edge[:, k, :], hot[:, k, :], start=begin, stop=end)
                return ins

            def degree():
                nc.tensor.matmul(p_win[:, 2, 0:W], ones[:, :], hot_sum[:, :], start=True, stop=True)

            def group(layer, n, after=()):
                pe.wait_ge(s_added, n + 1)
                for q in range(QUADS):
                    pe.wait_ge(s_hot, QUADS * n + (q + 1))
                    pe.wait_ge(s_gath[q], 16 * QS * n + 16 * QS)
                    if not layer:
                        pe.wait_ge(s_edge[q], 16 * n + 16)
                    if q == QUADS - 1 and not layer:
                        pe.wait_ge(s_hot_sum, n + 2)
                        degree()
                    for k in range(q * QS, (q + 1) * QS):
                        ins = slot(layer, k)
                    ins.then_inc(s_used, 1)
                    for at, step in after:
                        if at == q:
                            step()

            def turn_in(layer, b):
                if not layer:
                    pe.wait_ge(n_row_in, 16 * b + 16)
                    for j in range(2):
                        ins = nc.tensor.transpose(p_in[:, j, 0:P], row_in[:, j, :], ident[:, :])
                    ins.then_inc(n_in, 1)

            def products(layer, b):
                pe.wait_ge(n_parts, b + (layer * BLOCKS + 1))
                for i, part in enumerate((mean, h_met, h_lone)):
                    ins = nc.tensor.matmul(p_node[:, 0:BLOCK], wT[:, 3 * layer + i, :], part[:, :],
                                           start=(i == 0), stop=(i == 2))
                ins.then_inc(n_prod, 1)

            def turn_out(layer, b):
                pe.wait_ge(n_act, b + (layer * BLOCKS + 1))
                pairs = act_out[:, :].rearrange("f (p j) -> f p j", j=2)
                for j in range(2):
                    ins = nc.tensor.transpose(p_out[:, j, 0:P], pairs[:, :, j], ident[:, :])
                ins.then_inc(n_out, 1)

            def whole_block(layer, b):
                turn_in(layer, b)
                products(layer, b)
                turn_out(layer, b)

            mixed_pe = None
            for layer in range(2):
                n0 = layer * GROUPS
                group(layer, n0)
                if not layer:
                    pe.wait_ge(s_wc, 2)
                    mixed_pe = general(pe)
                with pe.If(mixed_pe == 0):
                    with pe.Fori(1, 3) as g:
                        group(layer, g + n0)
                    with pe.Fori(1, PAIRS) as i:
                        turn_in(layer, i - 1)
                        group(layer, 2 * i + (n0 + 1), after=((1, lambda: products(layer, i - 1)),
                                                              (2, lambda: turn_out(layer, i - 1))))
                        group(layer, 2 * i + (n0 + 2))
                    for b in (BLOCKS - 2, BLOCKS - 1):
                        whole_block(layer, b)
                with pe.If(mixed_pe != 0):
                    with pe.Fori(1, GROUPS) as g:
                        group(layer, g + n0)
                    with pe.Fori(0, GROUPS) as g:
                        pe.wait_ge(x_gath, 16 * SLOTS * (g + (n0 + 1)))
                        if not layer:
                            pe.wait_ge(x_edge, 16 * g + 16)
                        mark(pe)
                        with pe.Fori(1, WINDOWS) as w:
                            m = (g + n0) * (WINDOWS - 1) + w
                            pe.wait_ge(x_hot, QUADS * m)
                            pe.wait_ge(x_added, m)
                            if not layer:
                                pe.wait_ge(x_hot_sum, m)
                                degree()
                            for k in range(SLOTS):
                                ins = slot(layer, k)
                            ins.then_inc(x_win, 1)
                    with pe.Fori(0, BLOCKS) as b:
                        whole_block(layer, b)


_INS = ['x', 'src', 'dst', 'edge_attr_128', 'L0_gnn_Wn0', 'L0_gnn_Ws0', 'L0_gnn_Wi0',
        'L0_gnn_Wn1', 'L0_gnn_Ws1', 'L0_gnn_Wi1']


def kernel(**inputs):
    import numpy as _np
    import concourse.bacc as _bacc
    from concourse import mybir as _mybir
    from concourse.bass_utils import run_bass_kernel_spmd as _run

    nc = _bacc.Bacc("TRN2", target_bir_lowering=False, num_devices=1)
    arrays, args = {}, []
    for name in _INS:
        a = _np.ascontiguousarray(inputs[name])
        arrays[f"in_{name}"] = a
        args.append(nc.dram_tensor(f"in_{name}", a.shape, _mybir.dt.from_np(a.dtype), kind="ExternalInput").ap())
    args.append(nc.dram_tensor("out_0", inputs['x'].shape, _mybir.dt.float32, kind="ExternalOutput").ap())
    gnn_program(nc, *args)
    r = _run(nc, [arrays], core_ids=[0])
    return r.results[0]["out_0"]
```

```python
import concourse.bass as bass
from concourse import mybir
from contextlib import ExitStack


def gnn_program(nc, x, src, dst, edge_attr, Wn0, Ws0, Wi0, Wn1, Ws1, Wi1, out):
    fp32 = mybir.dt.float32
    bf16 = mybir.dt.bfloat16
    i32 = mybir.dt.int32
    i16 = mybir.dt.int16
    ALU = mybir.AluOpType
    ACT = mybir.ActivationFunctionType
    AX = mybir.AxisListType
    ds = bass.ds

    P = 128
    NODES, D = x.shape
    EDGES = src.shape[0]
    W = 144
    WU = 128
    BLOCK = 256
    BLOCKS = -(-NODES // BLOCK)
    COLS = BLOCKS * BLOCK
    WINDOWS = -(-COLS // W)
    TABLE = WINDOWS * W
    TAIL_N = NODES - (BLOCKS - 1) * BLOCK
    NB = 5
    STEPS = BLOCKS // NB
    TILES = 2 * BLOCKS

    UNITS = 16
    CHUNKS = 14
    UNIT = P * CHUNKS
    SPAN = 4
    ALL_CHUNKS = UNITS * CHUNKS
    HALF = ALL_CHUNKS // 2
    CW = 14
    CODES = TILES * CW
    COUNTED = UNITS * UNIT

    SLOTS = 16
    QUADS = 4
    QS = SLOTS // QUADS
    GROUP = P * SLOTS
    FULL = (EDGES - COUNTED) // GROUP
    GROUPS = FULL + 1
    TAIL_P = (EDGES - COUNTED - FULL * GROUP) // SLOTS
    ROUNDS = UNITS // 2
    GATHERED = (GROUPS, GROUPS - ROUNDS)
    POSITIONS = (0, 2, 3)
    BUILT0 = ALL_CHUNKS
    BUILT = ROUNDS * SLOTS
    assert BUILT == P
    SLOPE = (1.0 / 8.0 + 1.0 / 3.0) / 2.0
    EPS = 1e-5
    FIRST_B = 8
    LAG = 3
    AT_END = [BLOCKS - 2, BLOCKS - 1, ROUNDS - LAG, ROUNDS - LAG + 1, FIRST_B - 1]
    BATCHES = ((0, 2), (2, 5))
    assert COUNTED + FULL * GROUP + TAIL_P * SLOTS == EDGES and 0 < TAIL_P <= P
    assert GROUPS == 3 + 4 * ROUNDS and FIRST_B + 2 * ROUNDS - 2 == BLOCKS - 3 and AT_END[4] == AT_END[3] + 1
    assert UNITS // 2 * CHUNKS == HALF and BLOCKS % NB == 0 and TAIL_N % 2 == 0

    G0, G1 = COUNTED, COUNTED + FULL * GROUP
    edge_full = edge_attr[G0:G1, :].rearrange("(g p k) d -> p g (k d)", p=P, k=SLOTS)
    edge_tail = edge_attr[G1:EDGES, :].rearrange("(p k) d -> p (k d)", k=SLOTS)
    edge_unit = edge_attr[0:COUNTED, :].rearrange("(u p k) d -> p u (k d)", p=P, k=CHUNKS)
    x_full = x[0:(BLOCKS - 1) * BLOCK, :].rearrange("(b p j) d -> p b (j d)", p=P, j=2)
    x_tail = x[(BLOCKS - 1) * BLOCK:NODES, :].rearrange("(p j) d -> p (j d)", j=2)
    out_full = out[0:(BLOCKS - 1) * BLOCK, :].rearrange("(b p j) d -> p b (j d)", p=P, j=2)
    out_tail = out[(BLOCKS - 1) * BLOCK:NODES, :].rearrange("(p j) d -> p (j d)", j=2)

    ctx = ExitStack()
    with ctx:
        def sb(name, shape, dt=fp32):
            return ctx.enter_context(nc.sbuf_tensor(name, shape, dt))

        def pb(name, shape):
            return ctx.enter_context(nc.psum_tensor(name, shape, fp32))

        def sem(name):
            return ctx.enter_context(nc.semaphore(name))

        h_dram = [nc.dram_tensor(f"h{layer}_rows", (COLS, D), fp32, kind="Internal").ap() for layer in range(2)]
        h_rows = [h.rearrange("(b p j) d -> p b (j d)", p=P, j=2) for h in h_dram]
        count_dram = nc.dram_tensor("count_units", (UNITS, P, TILES * WU), bf16, kind="Internal").ap()
        count_units = count_dram.rearrange("u p n -> p u n")

        sums = sb("sums", [P, 3, TABLE])
        x_sb = sums[:, 0, 0:COLS].rearrange("p (b n) -> p b n", n=2 * D)
        gath = sb("gath", [P, SLOTS, D])
        edge = sb("edge", [P, SLOTS, D])
        hot = sb("hot", [P, SLOTS, W])
        src_sb = sb("src_sb", [P, GROUPS, SLOTS], i32)
        dst_sb = sb("dst_sb", [P, GROUPS, SLOTS])
        idx = sb("idx", [P, SLOTS], i32)
        iota = sb("iota", [P, W])
        ones = sb("ones", [P, P])
        ones_b = sb("ones_b", [P, P], bf16)
        ident = sb("ident", [P, P])
        wT = sb("wT", [P, 6, D])

        u_space = sb("u_space", [P, max(CHUNKS * (D + WU), TILES * W // 2)])
        u_edge = u_space[:, 0:CHUNKS * D].rearrange("p (k d) -> p k d", d=D)
        u_hot = u_space[:, CHUNKS * D:CHUNKS * (D + WU)].rearrange("p (k w) -> p k w", w=WU)
        count_b = u_space[:, 0:TILES * W // 2].bitcast(bf16).rearrange("p (t w) -> p t w", w=W)
        x_in = edge[:, 10:12, :]
        y_rows = edge[:, 12:14, :]
        u_src = sb("u_src", [P, UNITS, CHUNKS], i32)
        u_dst = sb("u_dst", [P, UNITS, CHUNKS])
        count = sb("count", [P, 2, TILES, WU], bf16)
        c_off = sb("c_off", [1, ALL_CHUNKS + BUILT], i32)
        lane = sb("lane", [P, ALL_CHUNKS + BUILT + 2])
        code = sb("code", [P, ALL_CHUNKS + BUILT + 2])
        iota_lane = sb("iota_lane", [P, P], bf16)
        iota_code = sb("iota_code", [P, CODES], i16)
        lane_hot = sb("lane_hot", [P, 2, P], bf16)
        code_hot = sb("code_hot", [P, 2, CODES], bf16)

        base_i = sb("base_i", [1, GROUPS + UNITS], i32)
        mixed_i = sb("mixed_i", [1, 1], i32)

        row_in = sb("row_in", [P, 2, D])
        mean = sb("mean", [P, BLOCK])
        h_lone = sb("h_lone", [P, BLOCK])
        h_met = sb("h_met", [P, BLOCK])
        made = sb("made", [P, BLOCK])

        end_rows = gath[:, 0:10, :]
        end_x = edge[:, 0:10, :]
        in_hot = hot[:, :, :].rearrange("p k w -> p (k w)")
        in_u_hot = u_hot[:, :, :].rearrange("p k w -> p (k w)")
        in_u_edge = u_edge[:, 2:CHUNKS, :].rearrange("p k d -> p (k d)")

        def nth(buffer, i, count=1):
            return buffer[:, i * BLOCK:(i + count) * BLOCK]

        end_mean = [nth(in_hot, i) for i in range(5)]
        end_lone = [nth(in_hot, 5 + i) for i in range(3)] + [nth(in_u_hot, i) for i in range(2)]
        end_met = [nth(in_u_hot, 2 + i) for i in range(5)]
        end_made = [nth(in_u_edge, i) for i in range(5)]

        with ExitStack() as setup:
            def setup_sb(name, shape, dt=fp32):
                return setup.enter_context(nc.sbuf_tensor(name, shape, dt))

            setup_sb("first_part", [P, TILES, D], bf16)
            dst_i = setup_sb("dst_i", [P, GROUPS, SLOTS], i32)
            w_raw = setup_sb("w_raw", [P, 6, D])
            u_dst_i = setup_sb("u_dst_i", [P, UNITS, CHUNKS], i32)
            c_src = setup_sb("c_src", [HALF, 2, P], i32)
            c_dst = setup_sb("c_dst", [HALF, 2, P], i32)
            c_tmp = setup_sb("c_tmp", [HALF, 2, P], i32)
            c_tile = setup_sb("c_tile", [HALF, 2, P], i32)
            c_lane_f = setup_sb("c_lane_f", [HALF, 2, P])
            c_code_f = setup_sb("c_code_f", [HALF, 2, P])
            c_ends = setup_sb("c_ends", [HALF, 2, 2])
            c_row = setup_sb("c_row", [1, 2, ALL_CHUNKS])
            c_bad = setup_sb("c_bad", [1, 4, ALL_CHUNKS])
            b_src = setup_sb("b_src", [P, P], i32)
            b_dst = setup_sb("b_dst", [P, P], i32)
            b_tmp = setup_sb("b_tmp", [P, P], i32)
            b_tile = setup_sb("b_tile", [P, P], i32)
            b_lane_f = setup_sb("b_lane_f", [P, P])
            b_code_f = setup_sb("b_code_f", [P, P])
            b_ends = setup_sb("b_ends", [P, 2])
            b_row = setup_sb("b_row", [1, 2, BUILT])
            b_bad = setup_sb("b_bad", [1, 4, BUILT])
            ends_part = setup_sb("ends_part", [P, 2, GROUPS])
            ends_group = setup_sb("ends_group", [GROUPS, 2])
            ends = setup_sb("ends", [1, 2, GROUPS])
            bound = setup_sb("bound", [1, GROUPS + UNITS])
            excess = setup_sb("excess", [1, 2, GROUPS])
            bases = setup_sb("bases", [1, GROUPS + UNITS])
            base_all = setup_sb("base_all", [P, GROUPS + UNITS])
            worst = setup_sb("worst", [1, 8])
            mixed = setup_sb("mixed", [1, 2])
            stats = setup_sb("stats", [P, TILES, 6])
            mv = setup_sb("mv", [P, TILES, 2])
            std = setup_sb("std", [P, TILES])
            rstd = setup_sb("rstd", [P, TILES])
            shift = setup_sb("shift", [P, TILES])
            eps = setup_sb("eps", [P, 1])
        h_parts = sb("h_parts", [P, 3, TILES, D], bf16)

        p_main = pb("p_main", [P, 3, 512])
        p_blk = pb("p_blk", [P, 512])
        p_node = p_blk[:, 0:BLOCK]
        p_in = p_blk[:, BLOCK:512].rearrange("p (j n) -> p j n", j=2)
        p_out = p_in
        p_unit = pb("p_unit", [P, 512])
        p_prod = pb("p_prod", [P, 512])
        p_cnt = pb("p_cnt", [P, 2, 512])
        end_banks = [p_blk[:, :], p_unit[:, :], p_cnt[:, 0, :], p_cnt[:, 1, :], p_prod[:, :]]
        end_node = [bank[:, 0:BLOCK] for bank in end_banks]
        end_in = [bank[:, BLOCK:512].rearrange("p (j n) -> p j n", j=2) for bank in end_banks]

        s_x = [sem(f"s_x{c}") for c in range(STEPS)]
        s_x_pad = sem("s_x_pad")
        s_idx_pad = sem("s_idx_pad")
        s_dst = sem("s_dst")
        s_src = sem("s_src")
        s_chk = sem("s_chk")
        s_w = sem("s_w")
        s_ident0 = sem("s_ident0")
        s_ident = sem("s_ident")
        s_iota = sem("s_iota")
        s_zeroed = sem("s_zeroed")
        s_cleared = sem("s_cleared")
        s_cleared_act = sem("s_cleared_act")
        s_eps = sem("s_eps")
        s_ends_part = sem("s_ends_part")
        s_ends_t = sem("s_ends_t")
        s_ends_out = sem("s_ends_out")
        s_ends = sem("s_ends")
        s_bases = sem("s_bases")
        s_bases_t = sem("s_bases_t")
        s_chk_b = sem("s_chk_b")
        s_chk_part = sem("s_chk_part")
        s_chk_t = sem("s_chk_t")
        s_chk_out = sem("s_chk_out")
        s_chk_row = sem("s_chk_row")
        s_base = sem("s_base")
        s_wt = sem("s_wt")
        s_wc = sem("s_wc")
        s_mv = sem("s_mv")
        s_std = sem("s_std")
        s_shift = sem("s_shift")
        s_norm = sem("s_norm")
        s_h0 = sem("s_h0")
        s_part = [sem(f"s_part{n}") for n in range(3)]
        s_rest = [sem(f"s_rest{n}") for n in range(2)]
        s_chain = sem("s_chain")
        s_idx = sem("s_idx")
        s_gath = [sem(f"s_gath{q}") for q in range(QUADS)]
        s_edge = [sem(f"s_edge{q}") for q in range(QUADS)]
        s_hot = sem("s_hot")
        s_used = sem("s_used")
        s_added = sem("s_added")
        u_rows = sem("u_rows")
        u_hots = sem("u_hots")
        u_win = sem("u_win")
        u_win_added = sem("u_win_added")
        u_lane = sem("u_lane")
        u_code = sem("u_code")
        u_gap = sem("u_gap")
        u_cnt = sem("u_cnt")
        u_cnt_added = sem("u_cnt_added")
        u_zero = sem("u_zero")
        b_zero = sem("b_zero")
        u_stored = sem("u_stored")
        u_count = [sem(f"u_count{h}") for h in range(2)]
        u_prod = sem("u_prod")
        u_prod_added = sem("u_prod_added")
        x_idx = sem("x_idx")
        x_gath = [sem(f"x_gath{kind}") for kind in range(2)]
        x_edge = [sem(f"x_edge{kind}") for kind in range(2)]
        x_moved = sem("x_moved")
        x_hot = sem("x_hot")
        x_win = sem("x_win")
        x_added = sem("x_added")
        n_row_in = [sem(f"n_row_in{layer}") for layer in range(2)]
        n_end_rows = sem("n_end_rows")
        n_wide = sem("n_wide")
        n_in = sem("n_in")
        n_parts = sem("n_parts")
        n_prod = sem("n_prod")
        n_made = sem("n_made")
        n_act = sem("n_act")
        n_out = sem("n_out")
        n_rows = sem("n_rows")
        n_store = sem("n_store")
        s_mark = sem("s_mark")

        def mark(engine):
            engine.sem_inc(s_mark, 1)

        def general(engine):
            engine.wait_ge(s_base, 1)
            return engine.value_load(mixed_i[0:1, 0:1], min_val=0, max_val=1)

        def blocks_of(j, first):
            if first == 0:
                return [(FIRST_B, 0, 2)]
            if first is not None and first < LAG:
                return [(FIRST_B + 2 * j - 1, 2 * j - 1, 0), (FIRST_B + 2 * j, 2 * j, 2)]
            m = 3 * j + (2 * LAG - 1 - 3 * LAG)
            return [(FIRST_B + 2 * j - 1, m, 0), (j - LAG, m + 1, 1), (FIRST_B + 2 * j, m + 2, 2)]

        def blocks_1(j, first):
            if first == 0:
                return {1: (FIRST_B, 0)}
            if first is not None and first < LAG:
                return {0: (FIRST_B + 2 * j - 1, 2 * j - 1), 1: (FIRST_B + 2 * j, 2 * j)}
            m = 3 * j + (2 * LAG - 1 - 3 * LAG)
            found = {0: (FIRST_B + 2 * j - 1, m), 1: (FIRST_B + 2 * j, m + 1), 2: (j - LAG, m + 2)}
            if first is None:
                found[-1] = (j + (-LAG - 1), m - 1)
            return found

        def rounds_1(engine, round_):
            for j in range(LAG + 1):
                round_(j, first=j)
            with engine.Fori(LAG + 1, ROUNDS - 1) as j:
                round_(j)
            round_(ROUNDS - 1, last=True)

        CLEARED_BY_DVE = 3

        IN_ROUNDS = 2 * LAG - 1 + 3 * (ROUNDS - LAG)
        assert IN_ROUNDS + len(AT_END) == BLOCKS

        KINDS = ((GROUPS, SLOTS, 1), (UNITS, CHUNKS, 0))
        X_LAYER = GROUPS * (WINDOWS - 1) + UNITS * WINDOWS

        PRODUCTS = (UNITS, UNITS + 3 * ROUNDS)

        def x_start(layer, kind):
            return layer * X_LAYER + (GROUPS * (WINDOWS - 1) if kind else 0)

        block = ctx.enter_context(nc.Block())

        @block.sync
        def _(sp):
            for c in range(STEPS):
                if c < STEPS - 1:
                    sp.dma_start(x_sb[:, c * NB:(c + 1) * NB, :], x_full[:, c * NB:(c + 1) * NB, :]).then_inc(s_x[c], 16)
                else:
                    sp.dma_start(x_sb[:, c * NB:BLOCKS - 1, :], x_full[:, c * NB:BLOCKS - 1, :]).then_inc(s_x[c], 16)
                    sp.wait_ge(s_x_pad, 1)
                    sp.dma_start(x_sb[0:TAIL_N // 2, BLOCKS - 1, :], x_tail).then_inc(s_x[c], 16)
            for table, flat in ((b_dst, dst), (b_src, src)):
                for j in range(ROUNDS):
                    e = G0 + (SPAN * j + 4) * GROUP
                    sp.dma_start(table[j * SLOTS:(j + 1) * SLOTS, :], flat[e:e + GROUP].rearrange("(k e) -> k e", e=P)
                                 ).then_inc(s_chk_b, 16)
            for n, w in enumerate((Wn0, Ws0, Wi0, Wn1, Ws1, Wi1)):
                sp.dma_start(w_raw[:, n, :], w).then_inc(s_w, 16)
            for c in range(STEPS):
                sp.wait_ge(s_norm, c + 1)
                sp.dma_start(h_rows[0][:, c * NB:(c + 1) * NB, :], x_sb[:, c * NB:(c + 1) * NB, :]).then_inc(s_h0, 16)
            sp.wait_ge(s_h0, 16 * STEPS)

            def as_rows(buffer):
                return buffer[:, :, :].rearrange("p j d -> p (j d)")

            def load_rows(layer, b, last=False):
                sp.dma_start(as_rows(row_in), h_rows[layer][:, ds(b, 1), :].rearrange("p b n -> p (b n)")
                             ).then_inc(n_row_in[layer], 16)
                if layer and last:
                    sp.dma_start(x_in[0:TAIL_N // 2, :, :].rearrange("p j d -> p (j d)"), x_tail).then_inc(n_row_in[layer], 16)
                elif layer:
                    sp.dma_start(as_rows(x_in), x_full[:, ds(b, 1), :].rearrange("p b n -> p (b n)")
                                 ).then_inc(n_row_in[layer], 16)

            def load_edges(q, g, n):
                at = slice(q * QS * D, (q + 1) * QS * D)
                to = edge[:, q * QS:(q + 1) * QS, :].rearrange("p k d -> p (k d)")
                sp.wait_ge(s_used, QUADS * n + (q + 1))
                if g is None:
                    sp.dma_start(to[0:TAIL_P, :], edge_tail[:, at]).then_inc(s_edge[q], 16)
                else:
                    sp.dma_start(to, edge_full[:, ds(g, 1), at].rearrange("p g n -> p (g n)")).then_inc(s_edge[q], 16)

            def store_block(layer, b, i, last=False):
                m = i + layer * BLOCKS
                sp.wait_ge(n_rows, m + 1)
                if layer and last:
                    sp.dma_start(out_tail, y_rows[0:TAIL_N // 2, :, :].rearrange("p j d -> p (j d)")
                                 ).then_inc(n_store, 16)
                elif layer:
                    sp.dma_start(out_full[:, ds(b, 1), :].rearrange("p b n -> p (b n)"), as_rows(y_rows)
                                 ).then_inc(n_store, 16)
                else:
                    sp.dma_start(h_rows[1][:, ds(b, 1), :].rearrange("p b n -> p (b n)"),
                                 x_sb[:, ds(b, 1), :].rearrange("p b n -> p (b n)")).then_inc(n_store, 16)

            def unit_rows(u):
                sp.wait_ge(u_win, u + 1)
                sp.dma_start(u_edge[:, :, :].rearrange("p k d -> p (k d)"),
                             edge_unit[:, ds(u, 1), :].rearrange("p u n -> p (u n)")).then_inc(u_rows, 16)

            def counts_of(half):
                return count[:, half, :, :].rearrange("p t w -> p (t w)")

            def store_counts(u, half):
                sp.wait_ge(u_cnt_added, CHUNKS * u + (CHUNKS + 1))
                sp.dma_start(count_units[:, ds(u, 1), :].rearrange("p u n -> p (u n)"), counts_of(half)
                             ).then_inc(u_stored, 16)

            def load_counts(u, half, used=None):
                if used is not None:
                    sp.wait_ge(u_prod, used)
                sp.dma_start(counts_of(half), count_units[:, ds(u, 1), :].rearrange("p u n -> p (u n)")
                             ).then_inc(u_count[half], 16)

            def end_loads(layer):
                sp.wait_ge(s_used, QUADS * (sum(GATHERED[:layer + 1]) + 1))
                for i0, i1 in BATCHES:
                    b0 = AT_END[i0]
                    sp.dma_start(end_rows[:, 2 * i0:2 * i1, :].rearrange("p (b j) d -> p b (j d)", j=2),
                                 h_rows[layer][:, b0:b0 + i1 - i0, :]).then_inc(n_end_rows, 16)
                if layer:
                    for i in range(len(AT_END)):
                        to = end_x[:, 2 * i:2 * i + 2, :].rearrange("p k d -> p (k d)")
                        if AT_END[i] == BLOCKS - 1:
                            sp.dma_start(to[0:TAIL_N // 2, :], x_tail).then_inc(n_end_rows, 16)
                        else:
                            sp.dma_start(to, x_full[:, AT_END[i], :]).then_inc(n_end_rows, 16)

            def end_stores(layer):
                for i, b in enumerate(AT_END):
                    sp.wait_ge(n_rows, layer * BLOCKS + IN_ROUNDS + i + 1)
                    rows_out = end_x[:, 2 * i:2 * i + 2, :].rearrange("p k d -> p (k d)") if layer else x_sb[:, b, :]
                    if layer and b == BLOCKS - 1:
                        sp.dma_start(out_tail, rows_out[0:TAIL_N // 2, :]).then_inc(n_store, 16)
                    else:
                        sp.dma_start((out_full if layer else h_rows[1])[:, b, :], rows_out).then_inc(n_store, 16)
                sp.wait_ge(n_store, 16 * BLOCKS * (layer + 1))

            def round_(layer, j, first=None, last=False):
                steps = {4 * 0 + g: (b, i) for b, i, g in blocks_of(j, first)}
                order = [b for b, _, _ in blocks_of(j, first)]
                order.append(None if last else FIRST_B + 2 * j + 1)
                done = 0
                for gi in range(4):
                    for q in range(QUADS):
                        if not layer:
                            n = 4 * j + (3 + gi)
                            load_edges(q, None if last and gi == 3 else n, n)
                        if q == 2 and gi - 1 in steps:
                            b, i = steps[gi - 1]
                            done += 1
                            if not layer and order[done] is not None:
                                sp.wait_ge(n_rows, i + 1)
                                mark(sp)
                                load_rows(layer, order[done])
                            store_block(layer, b, i)
                            if layer and order[done] is not None:
                                load_rows(layer, order[done])
                    if not layer and gi in (0, 2):
                        u = 2 * j + gi // 2
                        if gi or first != 0:
                            store_counts(u - 1, 1 - gi // 2)
                        unit_rows(u)

            def round_1(j, first=None, last=False):
                blocks = blocks_1(j, first)
                for pos in range(3):
                    if pos - 1 in blocks:
                        b, i = blocks[pos - 1]
                        sp.wait_ge(n_rows, i + (BLOCKS + 1))
                        mark(sp)
                        if pos in blocks:
                            load_rows(1, blocks[pos][0])
                        elif not last:
                            load_rows(1, FIRST_B + 2 * j + 1)
                        store_block(1, b, i)
                    if pos == 0 and first != 0:
                        load_counts(2 * j + 1, 1, used=3 * j + UNITS)
                    if pos == 2 and not last:
                        load_counts(2 * j + 2, 0, used=3 * j + (UNITS + 2))

            sp.wait_ge(s_used, QUADS)
            for q in range(QUADS):
                load_edges(q, 0, 0)
            mixed_sp = general(sp)
            with sp.If(mixed_sp == 0):
                for layer in range(2):
                    if not layer:
                        with sp.Fori(1, 3) as g:
                            for q in range(QUADS):
                                load_edges(q, g, g)
                        load_rows(0, FIRST_B)
                        for j in range(LAG):
                            round_(0, j, first=j)
                        with sp.Fori(LAG, ROUNDS - 1) as j:
                            round_(0, j)
                        round_(0, ROUNDS - 1, last=True)
                    else:
                        load_rows(1, FIRST_B)
                        rounds_1(sp, round_1)
                        store_block(1, ROUNDS - 1 - LAG, IN_ROUNDS - 1)
                    end_loads(layer)
                    if not layer:
                        store_counts(UNITS - 1, 1)
                        sp.wait_ge(u_stored, 16 * UNITS)
                        load_counts(0, 0)
                    end_stores(layer)
                    if not layer:
                        load_counts(1, 1, used=UNITS)
            with sp.If(mixed_sp != 0):
                with sp.Fori(1, FULL) as g:
                    for q in range(QUADS):
                        load_edges(q, g, g)
                for q in range(QUADS):
                    load_edges(q, None, FULL)
                whole = edge[:, :, :].rearrange("p k d -> p (k d)")
                sp.wait_ge(s_used, QUADS * (GROUPS + 1))
                with sp.Fori(0, FULL) as g:
                    sp.wait_ge(x_win, g * (WINDOWS - 1) + 1)
                    sp.dma_start(whole, edge_full[:, ds(g, 1), :].rearrange("p g n -> p (g n)")).then_inc(x_edge[0], 16)
                sp.wait_ge(x_win, FULL * (WINDOWS - 1) + 1)
                sp.dma_start(whole[0:TAIL_P, :], edge_tail).then_inc(x_edge[0], 16)
                with sp.Fori(0, UNITS) as u:
                    sp.wait_ge(x_win, u * WINDOWS + (x_start(0, 1) + 1))
                    sp.dma_start(whole[:, 0:CHUNKS * D], edge_unit[:, ds(u, 1), :].rearrange("p u n -> p (u n)")
                                 ).then_inc(x_edge[1], 16)
                for layer in range(2):
                    load_rows(layer, 0)
                    with sp.Fori(0, BLOCKS - 2) as b:
                        store_block(layer, b, b)
                        load_rows(layer, b + 1)
                    store_block(layer, BLOCKS - 2, BLOCKS - 2)
                    load_rows(layer, BLOCKS - 1, last=True)
                    store_block(layer, BLOCKS - 1, BLOCKS - 1, last=True)
                    sp.wait_ge(n_store, 16 * BLOCKS * (layer + 1))

        @block.gpsimd
        def _(pool):
            pool.memset(x_sb[:, BLOCKS - 1, :], 0.0).then_inc(s_x_pad, 1)
            pool.memset(src_sb[:, FULL, :], 0).then_inc(s_idx_pad, 1)
            pool.memset(dst_i[:, FULL, :], -1).then_inc(s_idx_pad, 1)
            pool.memset(ident[:, :], 0.0).then_inc(s_ident0, 1)
            pool.memset(bound[:, 0:1], float((ROUNDS - LAG + 1) * BLOCK))
            pool.iota(bound[:, 1:GROUPS].rearrange("o (i k) -> o i k", k=2),
                      pattern=[[BLOCK, (GROUPS - 1) // 2], [0, 2]], base=(FIRST_B - 1) * BLOCK,
                      channel_multiplier=0, allow_small_or_imprecise_dtypes=True)
            pool.iota(bound[:, GROUPS:GROUPS + UNITS], pattern=[[BLOCK // 2, UNITS]], base=-3 * BLOCK // 2,
                      channel_multiplier=0, allow_small_or_imprecise_dtypes=True)
            pool.iota(iota[:, :], pattern=[[1, W]], base=0, channel_multiplier=0,
                      allow_small_or_imprecise_dtypes=True)
            pool.iota(iota_lane[:, :], pattern=[[1, P]], base=0, channel_multiplier=0,
                      allow_small_or_imprecise_dtypes=True)
            pool.iota(iota_code[:, :], pattern=[[1, CODES]], base=0, channel_multiplier=0,
                      allow_small_or_imprecise_dtypes=True).then_inc(s_iota, 1)
            pool.wait_ge(s_ident0, 1)
            pool.affine_select(out=ident[:, :], in_=ident[:, :], compare_op=ALU.not_equal, fill=1.0,
                               base=0, pattern=[[-1, P]], channel_multiplier=1).then_inc(s_ident, 1)
            pool.memset(sums[:, 1:3, :], 0.0)
            pool.memset(sums[:, 0, COLS:TABLE], 0.0)
            pool.memset(lane[:, ALL_CHUNKS + BUILT:], 0.0)
            pool.memset(code[:, ALL_CHUNKS + BUILT:], 0.0)
            pool.memset(count[:, :, :, :], 0.0).then_inc(s_zeroed, 1)
            top = pool.to_reg(COLS - 1)

            def gather(layer, k, s_done):
                pool.indirect_dma_start(
                    out=gath[:, k, :], out_offset=None, in_=h_dram[layer][:, :],
                    in_offset=bass.IndirectOffsetOnAxis(ap=idx[:, k:k + 1], axis=0),
                    bounds_check=top, oob_is_err=False).then_inc(s_done, 16)

            def gather_groups(layer, groups):
                with pool.Fori(0, groups) as g:
                    for q in range(QUADS):
                        pool.wait_ge(s_idx, QUADS * g + (QUADS * GROUPS * layer + q + 1))
                        mark(pool)
                        for k in range(q * QS, (q + 1) * QS):
                            gather(layer, k, s_gath[q])

            pool.wait_ge(s_h0, 16 * STEPS)
            mixed_pool = None
            for layer in range(2):
                if layer:
                    pool.wait_ge(n_store, 16 * BLOCKS)
                    with pool.If(mixed_pool == 0):
                        gather_groups(layer, GATHERED[1])
                    with pool.If(mixed_pool != 0):
                        gather_groups(layer, GROUPS)
                else:
                    gather_groups(layer, GROUPS)
                    mixed_pool = general(pool)
                with pool.If(mixed_pool != 0):
                    for kind, (items, slots, _) in enumerate(KINDS):
                        with pool.Fori(0, items) as g:
                            pool.wait_ge(x_idx, g + (layer * (GROUPS + UNITS) + kind * GROUPS + 1))
                            mark(pool)
                            for k in range(slots):
                                gather(layer, k, x_gath[kind])

        @block.scalar
        def _(act):
            act.wait_ge(s_idx_pad, 2)
            for table, unit_table, flat, s_loaded in ((dst_i, u_dst_i, dst, s_dst), (src_sb, u_src, src, s_src)):
                act.dma_start(table[:, 0:FULL, :], flat[G0:G1].rearrange("(g p k) -> p g k", p=P, k=SLOTS)
                              ).then_inc(s_loaded, 16)
                act.dma_start(table[0:TAIL_P, FULL, :], flat[G1:EDGES].rearrange("(p k) -> p k", k=SLOTS)
                              ).then_inc(s_loaded, 16)
                act.dma_start(unit_table[:, :, :], flat[0:COUNTED].rearrange("(u p k) -> p u k", p=P, k=CHUNKS)
                              ).then_inc(s_loaded, 16)
            for table, flat in ((c_dst, dst), (c_src, src)):
                act.dma_start(table[:, :, :], flat[0:COUNTED].rearrange("(h q e) -> q h e", h=2, e=P)).then_inc(s_chk, 16)

            def std_of(c):
                tiles = slice(2 * NB * c, 2 * NB * (c + 1))
                act.wait_ge(s_mv, c + 1)
                act.activation(std[:, tiles], mv[:, tiles, 1], ACT.Sqrt, bias=eps[:, :]).then_inc(s_std, 1)

            act.wait_ge(s_eps, 1)
            std_of(0)
            for c in range(STEPS):
                if c + 1 < STEPS:
                    std_of(c + 1)
                act.wait_ge(s_shift, c + 1)
                for t in range(2 * NB * c, 2 * NB * (c + 1)):
                    row = x_sb[:, t // 2, (t % 2) * D:(t % 2 + 1) * D]
                    ins = act.activation(row, row, ACT.Relu, bias=shift[:, t:t + 1], scale=rstd[:, t:t + 1])
                ins.then_inc(s_norm, 1)

            def indices(q, g, n):
                act.wait_ge(s_used, QUADS * n + (q + 1))
                act.activation(idx[:, q * QS:(q + 1) * QS],
                               src_sb[:, ds(g, 1), q * QS:(q + 1) * QS].rearrange("p g k -> p (g k)"),
                               ACT.Copy).then_inc(s_idx, 1)

            def product_out(m, node=p_node, to=made[:, :]):
                act.wait_ge(n_prod, m + 1)
                act.activation(to, node, ACT.Copy).then_inc(n_made, 1)

            def part_of_h(layer, part, c):
                if part:
                    act.wait_ge(s_rest[part - 1], layer * STEPS + c + 1)
                act.activation(h_parts[:, part, 2 * NB * c:2 * NB * (c + 1), :].rearrange("p t d -> p (t d)"),
                               x_sb[:, NB * c:NB * (c + 1), :].rearrange("p b n -> p (b n)"),
                               ACT.Copy).then_inc(s_part[part], 1)

            def code_hots(c, half):
                act.wait_ge(u_cnt, c + 1)
                act.activation(code_hot[:, half, :], iota_code[:, :], ACT.Abs, bias=code[:, ds(c, 1)]).then_inc(u_gap, 1)
                act.wait_ge(u_gap, c + 1)
                act.activation(code_hot[:, half, :], code_hot[:, half, :], ACT.Relu, bias=1.0, scale=-1.0).then_inc(u_code, 1)

            def unit_step(u, s, half, first=False, last=False):
                if s < 7:
                    for h in range(2):
                        code_hots(CHUNKS * u + (2 * s + h + 2), h)
                if s >= 5 and not last:
                    if s == 5 and first:
                        act.wait_ge(s_zeroed, 1)
                    elif s == 5:
                        act.wait_ge(u_prod, u)
                        act.wait_ge(u_stored, 16 * u)
                    third = count[:, 1 - half, (s - 5) * TILES // 3:(s - 4) * TILES // 3, :].rearrange("p t w -> p (t w)")
                    act.activation(third, third, ACT.Copy, scale=0.0).then_inc(u_zero, 1)

            def round_(layer, j, first=None):
                n0, m0 = layer * GROUPS, layer * BLOCKS
                outs = {g + 1: i for _, i, g in blocks_of(j, first)}
                for gi in range(4):
                    n = 4 * j + (3 + gi)
                    for q in range(QUADS):
                        indices(q, n, n + n0)
                        if q == 1 and gi in outs:
                            product_out(outs[gi] + m0)
                        if not layer and (gi or first != 0):
                            unit_step(2 * j + (gi - 1) // 2, (gi - 1) % 2 * 4 + q, (gi - 1) // 2 % 2,
                                      first=(first == 0 and gi in (1, 2)))

            def round_1(j, first=None, last=False):
                blocks = blocks_1(j, first)
                for pos, gi in enumerate(POSITIONS):
                    for q in range(QUADS):
                        indices(q, 4 * j + (3 + gi), 3 * j + (GROUPS + 3 + pos))
                        if q == 1 and pos - 1 in blocks:
                            product_out(blocks[pos - 1][1] + BLOCKS)
                        for h in range(2):
                            if pos == 0:
                                code_hots(SLOTS * j + (BUILT0 + 10 + 2 * q + h), h)
                            if pos == 2 and not last:
                                code_hots(SLOTS * j + (BUILT0 + SLOTS + 2 + 2 * q + h), h)

            act.wait_ge(s_src, 48)
            mixed_act = None
            for layer in range(2):
                n0, m0 = layer * GROUPS, layer * BLOCKS
                for q in range(QUADS):
                    indices(q, 0, n0)
                if not layer:
                    mixed_act = general(act)
                with act.If(mixed_act == 0):
                    if layer:
                        act.wait_ge(n_rows, BLOCKS)
                    else:
                        act.wait_ge(s_h0, 16 * STEPS)
                        for part in range(3):
                            if part == 1:
                                act.wait_ge(s_wc, 2)
                            if part == 2:
                                for q in range(QUADS):
                                    indices(q, 1, 1)
                            for c in range(STEPS):
                                part_of_h(0, part, c)
                        for c in range(CLEARED_BY_DVE, STEPS):
                            piece = x_sb[:, NB * c:NB * (c + 1), :].rearrange("p b n -> p (b n)")
                            act.activation(piece, piece, ACT.Copy, scale=0.0).then_inc(s_cleared_act, 1)
                    for g in range(1, 3):
                        for q in range(QUADS):
                            if layer or g > 1:
                                indices(q, g, g + n0)
                            if layer:
                                for part in range(3):
                                    c = QUADS * (g - 1) + q - part
                                    if 0 <= c < STEPS:
                                        part_of_h(1, part, c)
                                if g == 2:
                                    for h in range(2):
                                        code_hots(BUILT0 + 2 + 2 * q + h, h)
                    if not layer:
                        act.wait_ge(s_chk_out, 1)
                        for h in range(2):
                            code_hots(h, h)
                        for j in range(LAG):
                            round_(0, j, first=j)
                        with act.Fori(LAG, ROUNDS) as j:
                            round_(0, j)
                        for s in range(4, 8):
                            unit_step(UNITS - 1, s, 1, last=True)
                    else:
                        rounds_1(act, round_1)
                        product_out(IN_ROUNDS - 1 + BLOCKS)
                    for i in range(len(AT_END)):
                        product_out(IN_ROUNDS + i + m0, end_node[i], end_made[i])
                with act.If(mixed_act != 0):
                    with act.Fori(1, GROUPS) as g:
                        for q in range(QUADS):
                            indices(q, g, g + n0)
                    act.wait_ge(s_used, QUADS * (n0 + GROUPS + 1))
                    for kind, (items, slots, w0) in enumerate(KINDS):
                        table = (src_sb, u_src)[kind]
                        with act.Fori(0, items) as g:
                            act.wait_ge(x_win, g * (WINDOWS - w0) + (x_start(layer, kind) + 1))
                            act.activation(idx[:, 0:slots], table[:, ds(g, 1), :].rearrange("p g k -> p (g k)"),
                                           ACT.Copy).then_inc(x_idx, 1)
                    with act.Fori(0, BLOCKS) as b:
                        product_out(b + m0)

        @block.vector
        def _(dve):
            chain = [0]

            def link(ins):
                chain[0] += 1
                ins.then_inc(s_chain, 1)
                dve.wait_ge(s_chain, chain[0])

            for s_credit in (s_added, u_win_added, u_cnt_added, u_prod_added, x_added):
                dve.sem_inc(s_credit, 1)
            dve.memset(eps[:, :], EPS).then_inc(s_eps, 1)
            dve.memset(ones_b[:, :], 1.0)
            link(dve.memset(ones[:, :], 1.0))

            def moments(c):
                dve.wait_ge(s_x[c], 32 if c == STEPS - 1 else 16)
                for t in range(2 * NB * c, 2 * NB * (c + 1)):
                    ins = dve.bn_stats(stats[:, t, :], x_sb[:, t // 2, (t % 2) * D:(t % 2 + 1) * D])
                link(ins)
                for t in range(2 * NB * c, 2 * NB * (c + 1)):
                    ins = dve.bn_aggr(mv[:, t, :], stats[:, t, :])
                ins.then_inc(s_mv, 1)

            def group_ends():
                dve.wait_ge(s_dst, 48)
                link(dve.tensor_copy(dst_sb[:, :, :], dst_i[:, :, :]))
                link(dve.tensor_reduce(ends_part[:, 1, :], dst_sb[:, :, :], AX.X, ALU.max))
                link(dve.tensor_scalar(dst_sb[:, FULL, :], dst_sb[:, FULL, :], 0.0, float(2 * TABLE), ALU.is_lt, ALU.mult))
                link(dve.tensor_tensor(dst_sb[:, FULL, :], dst_sb[:, FULL, :], dst_i[:, FULL, :], ALU.add))
                dve.tensor_reduce(ends_part[:, 0, :], dst_sb[:, :, :], AX.X, ALU.min).then_inc(s_ends_part, 1)

            moments(0)
            for c in range(STEPS):
                if c + 1 < STEPS:
                    moments(c + 1)
                else:
                    group_ends()
                tiles = slice(2 * NB * c, 2 * NB * (c + 1))
                dve.wait_ge(s_std, c + 1)
                link(dve.reciprocal(rstd[:, tiles], std[:, tiles]))
                dve.scalar_tensor_tensor(shift[:, tiles], mv[:, tiles, 0], -1.0, rstd[:, tiles],
                                         ALU.mult, ALU.mult).then_inc(s_shift, 1)

            dve.wait_ge(s_chk, 32)
            link(dve.tensor_copy(u_dst[:, :, :], u_dst_i[:, :, :]))
            built = [t[:, :].unsqueeze(1) for t in (b_src, b_dst, b_tmp, b_tile, b_lane_f, b_code_f)]
            counted = [t[:, :, :] for t in (c_src, c_dst, c_tmp, c_tile, c_lane_f, c_code_f)]
            dve.wait_ge(s_chk_b, 2 * 16 * ROUNDS)
            for (_, c_d, _, _, _, code_f), least, most in ((counted, c_ends[:, 0, :], c_ends[:, 1, :]),
                                                          (built, b_ends[:, 0:1], b_ends[:, 1:2])):
                link(dve.tensor_copy(code_f, c_d))
                link(dve.tensor_reduce(least, code_f, AX.X, ALU.min))
                dve.tensor_reduce(most, code_f, AX.X, ALU.max).then_inc(s_chk_part, 1)
            for (c_s, _, tmp, tile, lane_f, code_f), least in ((counted, c_ends[:, 0, :]), (built, b_ends[:, 0:1])):
                rows_, parts_ = c_s.shape[0], c_s.shape[1]
                link(dve.tensor_scalar(tmp, c_s, 1, 127, ALU.arith_shift_right, ALU.bitwise_and))
                dve.tensor_copy(lane_f, tmp)
                link(dve.tensor_scalar(tile, c_s, 8, 1, ALU.arith_shift_right, ALU.logical_shift_left))
                link(dve.tensor_scalar(tmp, c_s, 1, None, ALU.bitwise_and))
                dve.tensor_tensor(code_f, least.unsqueeze(2).broadcast_to([rows_, parts_, P]), code_f, ALU.subtract)
                link(dve.tensor_tensor(tile, tile, tmp, ALU.add))
                dve.scalar_tensor_tensor(code_f, tile, float(-CW), code_f, ALU.mult, ALU.add).then_inc(s_chk_part, 1)

            for i, op in enumerate((ALU.min, ALU.max)):
                dve.wait_ge(s_ends_t, i + 1)
                dve.tensor_reduce(ends_group[:, i:i + 1], p_cnt[0:GROUPS, i, 0:P], AX.X, op).then_inc(s_ends_out, 1)
            dve.wait_ge(s_ends, 1)
            link(dve.tensor_copy(ends[:, :, :], p_blk[0:1, 0:2 * GROUPS].rearrange("o (i g) -> o i g", i=2)))
            dve.wait_ge(s_chk_row, 1)
            link(dve.tensor_copy(c_row[:, :, :], p_unit[0:1, 0:2 * ALL_CHUNKS].rearrange("o (i c) -> o i c", i=2)))
            link(dve.tensor_copy(b_row[:, :, :], p_main[0:1, 0, 0:2 * BUILT].rearrange("o (i c) -> o i c", i=2)))
            dve.wait_ge(s_iota, 1)
            least, most = c_row[:, 0, :], c_row[:, 1, :]
            unit_least = least.rearrange("o (u c) -> o u c", c=CHUNKS)[:, :, 0:1]
            link(dve.tensor_copy(bases[:, GROUPS:GROUPS + UNITS], unit_least.rearrange("o u c -> o (u c)")))
            dve.scalar_tensor_tensor(excess[:, 0, :], ends[:, 1, :], float(1 - W), ends[:, 0, :], ALU.add, ALU.subtract)
            dve.tensor_tensor(excess[:, 1, :], bound[:, 0:GROUPS], ends[:, 0, :], ALU.subtract)
            for row, bad, each, width, off in ((c_row, c_bad, CHUNKS, WU, c_off[:, 0:BUILT0]),
                                               (b_row, b_bad, SLOTS, W, c_off[:, BUILT0:])):
                def items(ap, each=each):
                    return ap.rearrange("o (u c) -> o u c", c=each)

                lo, hi = row[:, 0, :], row[:, 1, :]
                dve.scalar_tensor_tensor(bad[:, 0, :], hi, float(1 - CW), lo, ALU.add, ALU.subtract)
                dve.scalar_tensor_tensor(bad[:, 1, :], lo, 1.0, hi, ALU.add, ALU.subtract)
                if each == CHUNKS:
                    link(dve.tensor_tensor(bad[:, 2, 1:], hi[:, 0:ALL_CHUNKS - 1], lo[:, 1:], ALU.subtract))
                    link(dve.tensor_copy(bad[:, 2, 0:1], bad[:, 0, 0:1]))
                else:
                    link(dve.tensor_tensor(items(bad[:, 2, :])[:, :, 1:], items(hi)[:, :, 0:each - 1], items(lo)[:, :, 1:],
                                           ALU.subtract))
                    link(dve.tensor_copy(items(bad[:, 2, :])[:, :, 0:1], items(bad[:, 0, :])[:, :, 0:1]))
                link(dve.tensor_tensor(items(bad[:, 3, :]), items(lo),
                                       items(lo)[:, :, 0:1].broadcast_to([1, lo.shape[1] // each, each]), ALU.subtract))
                link(dve.tensor_copy(off, bad[:, 3, :]))
                link(dve.tensor_scalar(bad[:, 3, :], bad[:, 3, :], float(CW - width), None, ALU.add))
            link(dve.tensor_tensor(bound[:, GROUPS:GROUPS + UNITS], bound[:, GROUPS:GROUPS + UNITS],
                                   bases[:, GROUPS:GROUPS + UNITS], ALU.subtract))
            dve.tensor_reduce(worst[:, 0:1], excess[:, :, :].rearrange("o i g -> o (i g)"), AX.X, ALU.max)
            dve.tensor_reduce(worst[:, 1:2], c_bad[:, :, :].rearrange("o i c -> o (i c)"), AX.X, ALU.max)
            dve.tensor_reduce(worst[:, 4:5], b_bad[:, :, :].rearrange("o i c -> o (i c)"), AX.X, ALU.max)
            dve.tensor_reduce(worst[:, 2:3], bound[:, GROUPS:GROUPS + UNITS], AX.X, ALU.max)
            link(dve.tensor_scalar(worst[:, 3:4], most[:, ALL_CHUNKS - 1:ALL_CHUNKS], float(1 - FIRST_B * BLOCK), None,
                                   ALU.add))
            link(dve.tensor_reduce(mixed[:, 0:1], worst[:, 0:5], AX.X, ALU.max))
            link(dve.tensor_scalar(mixed[:, 0:1], mixed[:, 0:1], 0.5, None, ALU.is_gt))
            link(dve.tensor_scalar(mixed[:, 1:2], mixed[:, 0:1], -1.0, 1.0, ALU.mult, ALU.add))
            link(dve.tensor_copy(bases[:, 0:GROUPS], ends[:, 0, :]))
            link(dve.tensor_scalar(bases[:, :], bases[:, :], float(TABLE - W), mixed[:, 1:2], ALU.min, ALU.mult))
            dve.tensor_copy(base_i[:, :], bases[:, :]).then_inc(s_bases, 1)
            dve.tensor_copy(mixed_i[:, :], mixed[:, 0:1]).then_inc(s_base, 1)
            dve.wait_ge(s_bases_t, 1)
            link(dve.tensor_copy(base_all[:, :], p_prod[:, 0:GROUPS + UNITS]))
            dve.tensor_tensor(dst_sb[:, :, :], dst_sb[:, :, :],
                              base_all[:, 0:GROUPS].unsqueeze(2).broadcast_to([P, GROUPS, SLOTS]), ALU.subtract)
            link(dve.tensor_tensor(u_dst[:, :, :], u_dst[:, :, :],
                                   base_all[:, GROUPS:GROUPS + UNITS].unsqueeze(2).broadcast_to([P, UNITS, CHUNKS]),
                                   ALU.subtract))
            dve.wait_ge(s_zeroed, 1)

            def one_hots(to, table, k, g, s_ready):
                width = to.shape[2]
                dve.tensor_tensor(
                    to[:, k, :],
                    iota[:, 0:width].unsqueeze(1).broadcast_to([P, k.stop - k.start, width]),
                    table[:, ds(g, 1), k].rearrange("p g k -> p (g k)").unsqueeze(2).broadcast_to(
                        [P, k.stop - k.start, width]),
                    ALU.is_equal).then_inc(s_ready, 1)

            def add_window(layer, start, s_done):
                into = sums[:, 1, ds(start, W)] if layer else sums[:, :, ds(start, W)]
                dve.tensor_tensor(into, into, p_main[:, 0, 0:W] if layer else p_main[:, :, 0:W],
                                  ALU.add).then_inc(s_done, 1)

            def base_of(g):
                return dve.value_load(base_i[0:1, ds(g, 1)], min_val=0, max_val=TABLE - W)

            def add_group(layer, g, n):
                base = base_of(g)
                dve.wait_ge(s_used, QUADS * n + 2 * QUADS)
                add_window(layer, base, s_added)

            def group(layer, g, n, first=False, after=None, last_g=None, built_added=None, before=None):
                for q in range(QUADS):
                    if q == QUADS - 1 and not first:
                        if built_added is not None:
                            dve.wait_ge(u_prod_added, built_added)
                        add_group(layer, g - 1 if last_g is None else last_g, n - 1)
                    dve.wait_ge(s_used, QUADS * n + (q + 1))
                    if before:
                        before(q)
                    one_hots(hot, dst_sb, slice(q * QS, (q + 1) * QS), g, s_hot)
                    if after:
                        after(q)

            def lane_hots(c, half):
                dve.tensor_scalar(lane_hot[:, half, :], iota_lane[:, :], lane[:, ds(c, 1)], None,
                                  ALU.is_equal).then_inc(u_lane, 1)

            def add_counts(c, counts, h):
                off = dve.value_load(c_off[0:1, ds(c, 1)], min_val=0, max_val=counts.shape[2] - CW)
                dve.wait_ge(u_cnt, c + 3)
                into = counts[:, :, ds(off, CW)].rearrange("p (i t) w -> p i t w", i=2)
                dve.tensor_tensor(into, into, p_cnt[:, :, 0:CODES // 2].rearrange("p i (t w) -> p i t w", w=CW),
                                  ALU.add).then_inc(u_cnt_added, 1)
                lane_hots(c + 2, h)

            def add_product(layer, item, v, width=WU):
                base = base_of(item)
                dve.wait_ge(u_prod, v + 1)
                into = sums[:, layer, ds(base, width)]
                dve.tensor_tensor(into, into, p_prod[:, 0:width], ALU.add).then_inc(u_prod_added, 1)

            def add_unit_windows(u):
                base = base_of(u + GROUPS)
                dve.wait_ge(u_win, u + 2)
                into = sums[:, 1:3, ds(base, WU)]
                dve.tensor_tensor(into, into, p_unit[:, 0:2 * WU].rearrange("p (i w) -> p i w", i=2),
                                  ALU.add).then_inc(u_win_added, 1)

            def unit_start(u, s, half, first=False):
                if s < 7:
                    if s == 0 and not first:
                        add_unit_windows(u - 1)
                        dve.wait_ge(u_zero, 3 * u)
                        mark(dve)
                    add_counts(CHUNKS * u + 2 * s, count[:, half, :, :], 0)

            def unit_step(u, s, half, first=False):
                if s < 7:
                    one_hots(u_hot, u_dst, slice(2 * s, 2 * s + 2), u, u_hots)
                    add_counts(CHUNKS * u + (2 * s + 1), count[:, half, :, :], 1)
                if s == 5 and not first:
                    add_product(0, u + (GROUPS - 1), u - 1)

            def own_parts(layer, b, own, lone, met):
                rdeg = sums[:, 2, ds(b * BLOCK, BLOCK)].rearrange("f (p j) -> f p j", j=2)
                for to, op in ((lone, ALU.is_gt), (met, ALU.is_lt)):
                    ins = dve.scalar_tensor_tensor(to.rearrange("f (p j) -> f p j", j=2), rdeg, 1.5,
                                                   own.rearrange("f j p -> f p j"), op, ALU.mult)
                ins.then_inc(n_parts, 1)

            def mean_of(to, cols, total):
                return dve.scalar_tensor_tensor(to, sums[:, 2, cols], 1.0, total, ALU.min, ALU.mult)

            def parts(layer, b, i):
                m = i + layer * BLOCKS
                cols = ds(b * BLOCK, BLOCK)
                if layer:
                    mean_of(mean[:, :], cols, sums[:, 1, cols])
                else:
                    at = 3 * m + chain[0]
                    dve.tensor_scalar(sums[:, 2, cols], sums[:, 2, cols], 0.5, None, ALU.max).then_inc(s_chain, 1)
                    dve.tensor_tensor(mean[:, :], sums[:, 0, cols], sums[:, 1, cols], ALU.add).then_inc(s_chain, 1)
                    dve.wait_ge(s_chain, at + 2)
                    mark(dve)
                    dve.reciprocal(sums[:, 2, cols], sums[:, 2, cols]).then_inc(s_chain, 1)
                    dve.wait_ge(s_chain, at + 3)
                    mean_of(mean[:, :], cols, mean[:, :])
                dve.wait_ge(n_in, m + 1)
                own_parts(layer, b, p_in, h_lone[:, :], h_met[:, :])

            def leaky(layer, i, buffer=made[:, :]):
                dve.wait_ge(n_made, i + (layer * BLOCKS + 1))
                dve.scalar_tensor_tensor(buffer, buffer, SLOPE, buffer,
                                         ALU.mult, ALU.max).then_inc(n_act, 1)

            def rows(layer, b, i):
                dve.wait_ge(n_out, i + (layer * BLOCKS + 1))
                if layer:
                    dve.wait_ge(n_store, 16 * i + 16 * BLOCKS)
                    dve.tensor_tensor(y_rows[:, :, :], p_out, x_in[:, :, :], ALU.add).then_inc(n_rows, 1)
                else:
                    mark(dve)
                    dve.tensor_copy(x_sb[:, ds(b, 1), :].rearrange("p b (j d) -> p (b j) d", j=2), p_out
                                    ).then_inc(n_rows, 1)

            def end_cols(batch):
                i0, i1 = BATCHES[batch]
                return slice(AT_END[i0] * BLOCK, (AT_END[i0] + i1 - i0) * BLOCK)

            def end_rdegs():
                for batch in range(2):
                    cols = end_cols(batch)
                    dve.tensor_scalar(sums[:, 2, cols], sums[:, 2, cols], 0.5, None, ALU.max).then_inc(n_wide, 1)
                for batch in range(2):
                    cols = end_cols(batch)
                    dve.wait_ge(n_wide, batch + 1)
                    dve.reciprocal(sums[:, 2, cols], sums[:, 2, cols]).then_inc(n_wide, 1)

            def end_means(layer, batch):
                i0, i1 = BATCHES[batch]
                cols = end_cols(batch)
                means = nth(in_hot, i0, i1 - i0)
                if layer:
                    mean_of(means, cols, sums[:, 1, cols])
                else:
                    dve.tensor_tensor(means, sums[:, 0, cols], sums[:, 1, cols], ALU.add).then_inc(n_wide, 1)
                    dve.wait_ge(n_wide, 5 + batch)
                    mean_of(means, cols, means)

            def end_parts(layer, i):
                dve.wait_ge(n_in, layer * BLOCKS + IN_ROUNDS + i + 1)
                own_parts(layer, AT_END[i], end_in[i], end_lone[i], end_met[i])

            def end_rows_out(layer, i):
                dve.wait_ge(n_out, layer * BLOCKS + IN_ROUNDS + i + 1)
                if layer:
                    to = end_x[:, 2 * i:2 * i + 2, :]
                    dve.tensor_tensor(to, end_in[i], to, ALU.add).then_inc(n_rows, 1)
                else:
                    dve.tensor_copy(x_sb[:, AT_END[i], :].rearrange("p (j d) -> p j d", j=2), end_in[i]
                                    ).then_inc(n_rows, 1)

            def end_blocks(layer):
                def act_on(i):
                    leaky(layer, IN_ROUNDS + i, end_made[i])

                dve.wait_ge(s_added, sum(GATHERED[:layer + 1]) + 1)
                if not layer:
                    dve.wait_ge(u_win_added, UNITS + 1)
                    end_rdegs()
                end_means(layer, 0)
                end_parts(layer, 0)
                end_parts(layer, 1)
                add_product(layer, GROUPS + UNITS - 1, PRODUCTS[layer] - 1)
                act_on(0)
                dve.wait_ge(u_prod_added, PRODUCTS[layer] + 1)
                act_on(1)
                end_means(layer, 1)
                for i in range(2, 5):
                    end_parts(layer, i)
                end_rows_out(layer, 0)
                end_rows_out(layer, 1)
                for i in range(2, 5):
                    act_on(i)
                for i in range(2, 5):
                    end_rows_out(layer, i)

            def weights_out():
                for i in range(2):
                    dve.wait_ge(s_wt, i + 1)
                    dve.tensor_copy(wT[:, 3 * i:3 * i + 3, :],
                                    p_cnt[:, i, 0:3 * D].rearrange("p (n d) -> p n d", n=3)).then_inc(s_wc, 1)

            def codes_out():
                dve.wait_ge(s_chk_t, 1)
                dve.tensor_copy(lane[:, 0:BUILT0 + BUILT], p_cnt[:, 0, 0:BUILT0 + BUILT])
                link(dve.tensor_copy(code[:, 0:BUILT0 + BUILT], p_cnt[:, 1, 0:BUILT0 + BUILT]))
                dve.sem_inc(s_chk_out, 1)

            def rest_of_h(layer, part, c):
                dve.wait_ge(s_part[part], layer * STEPS + c + 1)
                piece = x_sb[:, NB * c:NB * (c + 1), :].rearrange("p b n -> p (b n)")
                dve.tensor_tensor(piece, piece, h_parts[:, part, 2 * NB * c:2 * NB * (c + 1), :].rearrange(
                    "p t d -> p (t d)"), ALU.subtract).then_inc(s_rest[part], 1)

            def round_(layer, j, first=None):
                n0 = layer * GROUPS
                todo = blocks_of(j, first)
                at_group = {g: (b, i) for b, i, g in todo}
                for gi in range(4):
                    n = 4 * j + (3 + gi)

                    def before(q, gi=gi):
                        if gi or first != 0:
                            unit_start(2 * j + (gi - 1) // 2, (gi - 1) % 2 * 4 + q, (gi - 1) // 2 % 2,
                                       first=(first == 0 and gi in (1, 2)))

                    def after(q, gi=gi):
                        if gi - 1 in at_group and q == 1:
                            leaky(layer, at_group[gi - 1][1])
                        if gi - 1 in at_group and q == 2:
                            rows(layer, *at_group[gi - 1])
                        if not layer and (gi or first != 0):
                            u = 2 * j + (gi - 1) // 2
                            unit_step(u, (gi - 1) % 2 * 4 + q, (gi - 1) // 2 % 2, first=(first == 0 and gi in (1, 2)))

                    group(layer, n, n + n0, after=after, before=before)
                    if gi in at_group:
                        dve.wait_ge(s_added, n + (n0 + 1))
                        parts(layer, *at_group[gi])

            def clear_built(half):
                dve.memset(count_b[:, half * (TILES // 2):(half + 1) * (TILES // 2), :], 0.0).then_inc(b_zero, 1)

            def add_built(c, hs=(0, 1)):
                for h in hs:
                    add_counts(c + h, count_b, h)

            def round_1(j, first=None, last=False):
                blocks = blocks_1(j, first)
                for pos, gi in enumerate(POSITIONS):
                    g, n = 4 * j + (3 + gi), 3 * j + (GROUPS + 3 + pos)

                    def before(q, pos=pos):
                        if pos == 0:
                            add_built(SLOTS * j + (BUILT0 + 8 + 2 * q), (0,))
                        if pos == 2 and not last:
                            if q == 0:
                                dve.wait_ge(b_zero, 2 * j + 4)
                                mark(dve)
                            add_built(SLOTS * j + (BUILT0 + SLOTS + 2 * q), (0,))

                    def after(q, pos=pos, n=n):
                        if pos - 1 in blocks and q == 1:
                            leaky(1, blocks[pos - 1][1])
                        if pos - 1 in blocks and q == 2:
                            rows(1, *blocks[pos - 1])
                        if pos == 0:
                            add_built(SLOTS * j + (BUILT0 + 8 + 2 * q), (1,))
                        if pos == 2 and not last:
                            add_built(SLOTS * j + (BUILT0 + SLOTS + 2 * q), (1,))
                        if q == 2 and pos == 1:
                            dve.wait_ge(s_added, n)
                            add_product(1, 4 * j + 4, 3 * j + UNITS, W)
                            if not last:
                                clear_built(0)
                        if q == 3:
                            if pos == 0 and first != 0:
                                add_product(1, 2 * j + (GROUPS - 1), 3 * j + (UNITS - 1))
                            if pos == 1 and not last:
                                clear_built(1)
                            if pos == 2:
                                add_product(1, 2 * j + GROUPS, 3 * j + (UNITS + 1))

                    group(1, g, n, after=after, before=before, last_g=4 * j + 3 if pos == 1 else None,
                          built_added=3 * j + (UNITS + 2) if pos == 1 else None)
                    if pos in blocks:
                        dve.wait_ge(s_added, n + 1)
                        if pos == 1:
                            dve.wait_ge(u_prod_added, 3 * j + (UNITS + 2))
                        parts(1, *blocks[pos])

            mixed_dve = None
            for layer in range(2):
                n0 = layer * GROUPS
                if not layer:
                    codes_out()
                    weights_out()
                group(layer, 0, n0, first=True)
                if not layer:
                    mixed_dve = general(dve)
                chained = chain[0]
                with dve.If(mixed_dve == 0):
                    if not layer:
                        for part in range(2):
                            for c in range(STEPS):
                                rest_of_h(0, part, c)
                        for h in range(2):
                            lane_hots(h, h)
                        for c in range(CLEARED_BY_DVE):
                            dve.wait_ge(s_part[2], c + 1)
                            dve.memset(x_sb[:, NB * c:NB * (c + 1), :], 0.0).then_inc(s_cleared, 1)
                        dve.wait_ge(s_cleared, CLEARED_BY_DVE)
                        dve.wait_ge(s_cleared_act, STEPS - CLEARED_BY_DVE)
                    else:
                        dve.wait_ge(n_store, 16 * BLOCKS)
                        clear_built(0)
                        clear_built(1)
                    for g in range(1, 3):

                        def split(q, g=g):
                            for part in range(2):
                                c = QUADS * (g - 1) + q - part
                                if layer and 0 <= c < STEPS:
                                    rest_of_h(1, part, c)
                            if layer and g == 2:
                                if q == 0:
                                    dve.wait_ge(b_zero, 2)
                                add_built(BUILT0 + 2 * q)

                        group(layer, g, g + n0, after=split)
                    if layer:
                        rounds_1(dve, round_1)
                        leaky(1, IN_ROUNDS - 1)
                        rows(1, ROUNDS - 1 - LAG, IN_ROUNDS - 1)
                    else:
                        for j in range(LAG):
                            round_(0, j, first=j)
                        with dve.Fori(LAG, ROUNDS) as j:
                            round_(0, j)
                        for s in range(4, 8):
                            unit_start(UNITS - 1, s, 1)
                            unit_step(UNITS - 1, s, 1)
                        add_unit_windows(UNITS - 1)
                    add_group(layer, GROUPS - 1, sum(GATHERED[:layer + 1]) - 1)
                    end_blocks(layer)
                with dve.If(mixed_dve != 0):
                    if not layer:
                        dve.wait_ge(s_h0, 16 * STEPS)
                        dve.memset(sums[:, 0, 0:COLS], 0.0).then_inc(s_cleared, 1)
                        dve.wait_ge(s_cleared, 1)
                    with dve.Fori(1, GROUPS) as g:
                        group(layer, g, g + n0)
                    add_group(layer, GROUPS - 1, n0 + GROUPS - 1)
                    dve.wait_ge(s_added, n0 + GROUPS + 1)
                    for kind, (items, slots, w0) in enumerate(KINDS):
                        table = (dst_sb, u_dst)[kind]
                        moves = x_start(layer, kind) + layer * (GROUPS + 2 * UNITS) + kind * GROUPS
                        per_item = WINDOWS - w0 + 1 + kind
                        with dve.Fori(0, items) as g:
                            here = table[:, ds(g, 1), :].rearrange("p g k -> p (g k)")
                            if kind:
                                dve.tensor_scalar(here, here, float(W), None, ALU.add).then_inc(x_moved, 1)
                                dve.wait_ge(x_moved, g * per_item + (moves + 1))
                                mark(dve)
                            with dve.Fori(0, WINDOWS - w0) as w:
                                m = g * (WINDOWS - w0) + w + x_start(layer, kind)
                                dve.tensor_scalar(here, here, float(-W), None, ALU.add).then_inc(x_moved, 1)
                                dve.wait_ge(x_moved, g * per_item + w + (moves + kind + 1))
                                one_hots(hot, table, slice(0, slots), g, x_hot)
                                dve.wait_ge(x_win, m + 2)
                                add_window(layer, (w + w0) * W, x_added)
                                dve.wait_ge(x_added, m + 2)
                            dve.tensor_scalar(here, here, float((WINDOWS - 1) * W), None, ALU.add).then_inc(x_moved, 1)
                            dve.wait_ge(x_moved, g * per_item + (moves + per_item))
                    with dve.Fori(0, BLOCKS) as b:
                        parts(layer, b, b)
                        leaky(layer, b)
                        rows(layer, b, b)
                assert chain[0] == chained

        @block.tensor
        def _(pe):
            pe.sem_inc(s_used, QUADS)
            pe.sem_inc(u_win, 1)
            pe.sem_inc(u_cnt, 2)
            pe.sem_inc(x_win, 1)
            pe.wait_ge(s_ident, 1)
            pe.wait_ge(s_ends_part, 1)
            for i in range(2):
                nc.tensor.transpose(p_cnt[0:GROUPS, i, 0:P], ends_part[:, i, :], ident[:, :]).then_inc(s_ends_t, 1)
            pe.wait_ge(s_chk_part, 2)
            for i in range(2):
                for h in range(2):
                    at = (2 * i + h) * HALF
                    nc.tensor.transpose(p_unit[0:1, at:at + HALF], c_ends[:, i, h:h + 1], ident[0:HALF, 0:HALF])
                ins = nc.tensor.transpose(p_main[0:1, 0, i * BUILT:(i + 1) * BUILT], b_ends[:, i:i + 1], ident[:, :])
            ins.then_inc(s_chk_row, 1)
            pe.wait_ge(s_ends_out, 2)
            for i in range(2):
                ins = nc.tensor.transpose(p_blk[0:1, i * GROUPS:(i + 1) * GROUPS], ends_group[:, i:i + 1],
                                          ident[0:GROUPS, 0:GROUPS])
            ins.then_inc(s_ends, 1)
            pe.wait_ge(s_chk_part, 4)
            for i, (table, b_table) in enumerate(((c_lane_f, b_lane_f), (c_code_f, b_code_f))):
                for h in range(2):
                    nc.tensor.transpose(p_cnt[:, i, h * HALF:(h + 1) * HALF], table[:, h, :], ident[0:HALF, 0:HALF])
                ins = nc.tensor.transpose(p_cnt[:, i, BUILT0:BUILT0 + BUILT], b_table[:, :], ident[:, :])
            ins.then_inc(s_chk_t, 1)
            pe.wait_ge(s_bases, 1)
            nc.tensor.matmul(p_prod[:, 0:GROUPS + UNITS], ones[0:1, :], bases[:, :], start=True,
                             stop=True).then_inc(s_bases_t, 1)

            def turn_weights():
                pe.wait_ge(s_w, 16 * 6)
                pe.wait_ge(s_chk_out, 1)
                for i in range(2):
                    for n in range(3):
                        ins = nc.tensor.transpose(p_cnt[:, i, n * D:(n + 1) * D], w_raw[:, 3 * i + n, :], ident[:, :])
                    ins.then_inc(s_wt, 1)

            def ones_of(hots, k):
                return hots[:, k, :].bitcast(bf16).rearrange("p (w t) -> p w t", t=2)[:, :, 1]

            def slot(layer, k, slots=SLOTS):
                begin, end = k == 0, k == slots - 1
                ins = nc.tensor.matmul(p_main[:, 0, 0:W], gath[:, k, :], hot[:, k, :], start=begin, stop=end)
                if not layer:
                    nc.tensor.matmul(p_main[:, 2, 0:W], ones_b[:, :], ones_of(hot, k), start=begin, stop=end)
                    ins = nc.tensor.matmul(p_main[:, 1, 0:W], edge[:, k, :], hot[:, k, :], start=begin, stop=end)
                return ins

            def group(layer, n, after=None):
                pe.wait_ge(s_added, n + 1)
                for q in range(QUADS):
                    pe.wait_ge(s_hot, QUADS * n + (q + 1))
                    pe.wait_ge(s_gath[q], 16 * QS * n + 16 * QS)
                    if not layer:
                        pe.wait_ge(s_edge[q], 16 * n + 16)
                    for k in range(q * QS, (q + 1) * QS):
                        ins = slot(layer, k)
                    ins.then_inc(s_used, 1)
                    if after:
                        after(q)

            def product(v, counts, t0, t1, ready=None):
                if t0 == 0:
                    pe.wait_ge(u_prod_added, v + 1)
                    pe.wait_ge(*ready)
                    mark(pe)
                for t in range(t0, t1):
                    for part in range(3):
                        ins = nc.tensor.matmul(p_prod[:, 0:counts.shape[2]], h_parts[:, part, t, :], counts[:, t, :],
                                               start=(t == 0 and part == 0), stop=(t == TILES - 1 and part == 2))
                if t1 == TILES:
                    ins.then_inc(u_prod, 1)

            def unit_product(u, half, s):
                product(u, count[:, half, :, :], TILES * s // 5, TILES * (s + 1) // 5,
                        (u_cnt_added, CHUNKS * u + (CHUNKS + 1)))

            def chunk(c, h):
                pe.wait_ge(u_lane, c + 1)
                pe.wait_ge(u_code, c + 1)
                pe.wait_ge(u_cnt_added, c + 1)
                for i in range(2):
                    ins = nc.tensor.matmul(p_cnt[:, i, 0:CODES // 2], lane_hot[:, h, :],
                                           code_hot[:, h, i * (CODES // 2):(i + 1) * (CODES // 2)],
                                           start=True, stop=True)
                ins.then_inc(u_cnt, 1)

            UNIT_EDGES = {5: range(0, 7), 6: range(7, 12), 7: range(12, CHUNKS)}

            def unit_step(u, s, half, first=False):
                if s < 7:
                    chunk(CHUNKS * u + 2 * s, 0)
                if s < 5 and not first:
                    unit_product(u - 1, 1 - half, s)
                if s == 5:
                    pe.wait_ge(u_rows, 16 * u + 16)
                    pe.wait_ge(u_win_added, u + 1)
                if s >= 5:
                    pe.wait_ge(u_hots, 7 * u + s)
                    for k in UNIT_EDGES[s]:
                        ins = nc.tensor.matmul(p_unit[:, 0:WU], u_edge[:, k, :], u_hot[:, k, :], start=(k == 0),
                                               stop=(k == CHUNKS - 1))
                if s < 7:
                    chunk(CHUNKS * u + (2 * s + 1), 1)
                else:
                    for k in range(CHUNKS):
                        ins = nc.tensor.matmul(p_unit[:, WU:2 * WU], ones_b[:, :], ones_of(u_hot, k), start=(k == 0),
                                               stop=(k == CHUNKS - 1))
                    ins.then_inc(u_win, 1)

            def turn_in(layer, i):
                loads = 16 * (layer + 1)
                pe.wait_ge(n_row_in[layer], loads * i + loads)
                turn(row_in, p_in)

            def turn(rows, to):
                for j in range(2):
                    ins = nc.tensor.transpose(to[:, j, :], rows[:, j, :], ident[:, :])
                ins.then_inc(n_in, 1)

            def products(layer, i, node=p_node, mean=mean, h_met=h_met, h_lone=h_lone):
                pe.wait_ge(n_parts, i + (layer * BLOCKS + 1))
                for n, part in enumerate((mean, h_met, h_lone)):
                    ins = nc.tensor.matmul(node, wT[:, 3 * layer + n, :], part[:, :], start=(n == 0), stop=(n == 2))
                ins.then_inc(n_prod, 1)

            def turn_out(layer, i, buffer=made, to=p_out):
                pe.wait_ge(n_act, i + (layer * BLOCKS + 1))
                pairs = buffer[:, :].rearrange("f (p j) -> f p j", j=2)
                for j in range(2):
                    ins = nc.tensor.transpose(to[:, j, :], pairs[:, :, j], ident[:, :])
                ins.then_inc(n_out, 1)

            def end_blocks(layer):
                def take(i):
                    turn(end_rows[:, 2 * i:2 * i + 2, :], end_in[i])

                def make(i):
                    products(layer, IN_ROUNDS + i, end_node[i], end_mean[i], end_met[i], end_lone[i])

                def give(i):
                    turn_out(layer, IN_ROUNDS + i, end_made[i], end_in[i])

                pe.wait_ge(n_end_rows, (2 + 7 * layer) * 16)
                pe.wait_ge(n_rows, layer * BLOCKS + IN_ROUNDS)
                if not layer:
                    pe.wait_ge(u_win_added, UNITS + 1)
                for i in range(4):
                    take(i)
                make(0)
                make(1)
                pe.wait_ge(u_prod_added, PRODUCTS[layer] + 1)
                take(4)
                give(0)
                give(1)
                for i in range(2, 5):
                    make(i)
                for i in range(2, 5):
                    give(i)

            def whole_block(layer, i):
                turn_in(layer, i)
                products(layer, i)
                turn_out(layer, i)

            def round_(layer, j, first=None):
                n0 = layer * GROUPS
                at_group = {g: i for _, i, g in blocks_of(j, first)}
                for gi in range(4):
                    if gi in at_group:
                        turn_in(layer, at_group[gi])

                    def after(q, gi=gi):
                        s = gi % 2 * 4 + q
                        if gi in at_group and q == 1:
                            products(layer, at_group[gi])
                        if gi in at_group and q == 2:
                            turn_out(layer, at_group[gi])
                        u = 2 * j + gi // 2
                        unit_step(u, s, gi // 2, first=(first == 0 and gi < 2))

                    group(layer, 4 * j + (n0 + 3 + gi), after=after)

            def round_1(j, first=None, last=False):
                blocks = blocks_1(j, first)
                for pos in range(3):
                    n = 3 * j + (GROUPS + 3 + pos)
                    counts = (count_b, count[:, 0, :, :], count[:, 1, :, :])[pos]
                    ready = ((u_cnt_added, SLOTS * j + (BUILT0 + SLOTS + 1)), (u_count[0], 16 * j + 16),
                             (u_count[1], 16 * j + 16))[pos]
                    if pos in blocks:
                        turn_in(1, blocks[pos][1])

                    def after(q, pos=pos, counts=counts, ready=ready):
                        if pos in blocks and q == 1:
                            products(1, blocks[pos][1])
                        if pos in blocks and q == 2:
                            turn_out(1, blocks[pos][1])
                        build = pos > 0 and not last
                        c = SLOTS * j + (BUILT0 + SLOTS + 8 * (pos - 1) + 2 * q)
                        if build:
                            chunk(c, 0)
                        if pos:
                            product(3 * j + (UNITS + pos), counts, TILES * q // 4, TILES * (q + 1) // 4, ready)
                        elif q < 3:
                            product(3 * j + UNITS, counts, TILES * q // 3, TILES * (q + 1) // 3, ready)
                        if build:
                            chunk(c + 1, 1)

                    group(1, n, after=after)

            mixed_pe = None
            for layer in range(2):
                n0 = layer * GROUPS
                if not layer:
                    turn_weights()
                    pe.wait_ge(s_wc, 2)
                group(layer, n0)
                if not layer:
                    mixed_pe = general(pe)
                with pe.If(mixed_pe == 0):
                    for g in range(1, 3):

                        def build(q, g=g):
                            for h in range(2):
                                chunk(BUILT0 + 8 * (g - 1) + 2 * q + h, h)

                        group(layer, g + n0, after=build if layer else None)
                    pe.wait_ge(s_part[2], STEPS * (layer + 1))
                    if layer:
                        rounds_1(pe, round_1)
                    else:
                        for j in range(LAG):
                            round_(0, j, first=j)
                        with pe.Fori(LAG, ROUNDS) as j:
                            round_(0, j)
                        for s in range(5):
                            unit_product(UNITS - 1, 1, s)
                    end_blocks(layer)
                with pe.If(mixed_pe != 0):
                    with pe.Fori(1, GROUPS) as g:
                        group(layer, g + n0)
                    for kind, (items, slots, w0) in enumerate(KINDS):
                        with pe.Fori(0, items) as g:
                            pe.wait_ge(x_gath[kind], 16 * slots * g + 16 * slots * (items * layer + 1))
                            if not layer:
                                pe.wait_ge(x_edge[kind], 16 * g + 16)
                            mark(pe)
                            with pe.Fori(0, WINDOWS - w0) as w:
                                m = g * (WINDOWS - w0) + w + x_start(layer, kind)
                                pe.wait_ge(x_hot, m + 1)
                                pe.wait_ge(x_added, m + 1)
                                for k in range(slots):
                                    ins = slot(layer, k, slots)
                                ins.then_inc(x_win, 1)
                    with pe.Fori(0, BLOCKS) as b:
                        whole_block(layer, b)


_INS = ['x', 'src', 'dst', 'edge_attr_128', 'L0_gnn_Wn0', 'L0_gnn_Ws0', 'L0_gnn_Wi0',
        'L0_gnn_Wn1', 'L0_gnn_Ws1', 'L0_gnn_Wi1']


def kernel(**inputs):
    import numpy as _np
    import concourse.bacc as _bacc
    from concourse import mybir as _mybir
    from concourse.bass_utils import run_bass_kernel_spmd as _run

    nc = _bacc.Bacc("TRN2", target_bir_lowering=False, num_devices=1)
    arrays, args = {}, []
    for name in _INS:
        a = _np.ascontiguousarray(inputs[name])
        arrays[f"in_{name}"] = a
        args.append(nc.dram_tensor(f"in_{name}", a.shape, _mybir.dt.from_np(a.dtype), kind="ExternalInput").ap())
    args.append(nc.dram_tensor("out_0", inputs['x'].shape, _mybir.dt.float32, kind="ExternalOutput").ap())
    gnn_program(nc, *args)
    r = _run(nc, [arrays], core_ids=[0])
    return r.results[0]["out_0"]
```
